# Optimizing a Trainium2 kernel written in Bass

```python
import numpy as np
import jax
import jax.numpy as jnp

def _softmax(x, axis=-1):
    return jax.nn.softmax(x, axis=axis)

def _gelu(x):
    return jax.nn.gelu(x, approximate=True)

def _silu(x):
    return jax.nn.silu(x)

def _sigmoid(x):
    return jax.nn.sigmoid(x)

def _layernorm(x, axis=-1, eps=1e-05):
    m = jnp.mean(x, axis=axis, keepdims=True)
    v = jnp.var(x, axis=axis, keepdims=True)
    return (x - m) / jnp.sqrt(v + eps)

def _scatter_add(tgt, idx, src, axis=0):
    return tgt.at[idx].add(src)

def _segment_sum(src, seg, n):
    return jax.ops.segment_sum(src, seg, n)
kernel_name = 'mk_gnn_resnorm_d2_gnn_r32_13396b'

def setup_inputs(seed: int=0):
    np.random.seed(seed)
    _w = jnp.asarray

    def _rec_inputs():
        import jax
        import jax.numpy as jnp
        _gk = jax.random.key(seed)
        x = -0.000202 + 1 * jax.random.normal(jax.random.fold_in(_gk, 1), (50000, 128), jnp.float32)
        src = jax.random.randint(jax.random.fold_in(_gk, 2), (50000,), 0, 50000, jnp.int32)
        dst = jnp.minimum((50000 * jax.random.uniform(jax.random.fold_in(_gk, 3), (50000,)) ** 2.0).astype(jnp.int32), 49999)
        _o = jnp.argsort(dst, stable=True)
        src = src[_o]
        dst = dst[_o]
        edge_attr_128 = -5.16925e-05 + 1.00005 * jax.random.normal(jax.random.fold_in(_gk, 12), (50000, 128), jnp.float32)
        edge_attr_64 = -5.16925e-05 + 1.00005 * jax.random.normal(jax.random.fold_in(_gk, 13), (50000, 64), jnp.float32)
        return (x, src, dst, edge_attr_128, edge_attr_64)
    x, src, dst, edge_attr_128, edge_attr_64 = _rec_inputs()

    def _L0_gnn_setup():
        import jax, jax.numpy as jnp
        import numpy as np
        N = 50000
        E = 25000
        F = 128
        key = jax.random.key(seed)
        ks = jax.random.split(key, 10)
        x = jax.random.normal(ks[0], (N, F), dtype=jnp.float32)
        edge_index = jax.random.randint(ks[1], (2, E), 0, N, dtype=jnp.int32)
        edge_attr = jax.random.normal(ks[2], (E, F), dtype=jnp.float32)
        u = jax.random.normal(ks[3], (1, F), dtype=jnp.float32)
        batch = jnp.zeros((N,), dtype=jnp.int32)
        s1 = 1.0 / np.sqrt(2 * F)
        s2 = 1.0 / np.sqrt(F)
        W1 = jax.random.uniform(ks[4], (2 * F, F), jnp.float32, -s1, s1)
        b1 = jax.random.uniform(ks[5], (F,), jnp.float32, -s1, s1)
        W2 = jax.random.uniform(ks[6], (F, F), jnp.float32, -s2, s2)
        b2 = jax.random.uniform(ks[7], (F,), jnp.float32, -s2, s2)
        W3 = jax.random.uniform(ks[8], (F, F), jnp.float32, -s2, s2)
        b3 = jax.random.uniform(ks[9], (F,), jnp.float32, -s2, s2)
        return {'x': x, 'edge_index': edge_index, 'edge_attr': edge_attr, 'u': u, 'batch': batch, 'W1': W1, 'b1': b1, 'W2': W2, 'b2': b2, 'W3': W3, 'b3': b3}
    _L0_gnn_all = _L0_gnn_setup()
    _L0_gnn_in = {k: v for k, v in _L0_gnn_all.items() if k in ('u', 'W1', 'b1', 'W2', 'b2', 'W3', 'b3')}
    del _L0_gnn_all

    def _L1_gnn_setup():
        import jax, jax.numpy as jnp
        import numpy as np
        N_NODES = 50000
        N_EDGES = 50000
        F_NODE = 128
        F_EDGE = 64
        L = 128
        EPS = 1e-05

        def _bn(h, gamma, beta):
            mu = jnp.mean(h, axis=0, keepdims=True)
            var = jnp.mean((h - mu) ** 2, axis=0, keepdims=True)
            return (h - mu) * jax.lax.rsqrt(var + EPS) * gamma + beta
        key = jax.random.key(seed)
        ks = jax.random.split(key, 12)
        e1 = F_NODE + F_EDGE
        e2 = F_NODE + L
        inp = {'x': jax.random.normal(ks[0], (N_NODES, F_NODE), jnp.float32), 'edge_index': jax.random.randint(ks[1], (2, N_EDGES), 0, N_NODES, jnp.int32), 'edge_attr': jax.random.normal(ks[2], (N_EDGES, F_EDGE), jnp.float32), 'u': jax.random.normal(ks[3], (1, 4), jnp.float32), 'batch': jnp.zeros((N_NODES,), jnp.int32), 'W1': jax.random.normal(ks[4], (e1, L), jnp.float32) / np.sqrt(e1), 'b1': jnp.zeros((L,), jnp.float32), 'g1': jnp.ones((L,), jnp.float32), 'be1': jnp.zeros((L,), jnp.float32), 'W2': jax.random.normal(ks[5], (e2, e2), jnp.float32) / np.sqrt(e2), 'b2': jnp.zeros((e2,), jnp.float32), 'g2': jnp.ones((e2,), jnp.float32), 'be2': jnp.zeros((e2,), jnp.float32), 'Wl': jax.random.normal(ks[6], (e2, F_NODE), jnp.float32) / np.sqrt(e2), 'bl': jnp.zeros((F_NODE,), jnp.float32)}
        return inp
    _L1_gnn_all = _L1_gnn_setup()
    _L1_gnn_in = {k: v for k, v in _L1_gnn_all.items() if k in ('u', 'W1', 'b1', 'g1', 'be1', 'W2', 'b2', 'g2', 'be2', 'Wl', 'bl')}
    del _L1_gnn_all
    return {'x': x, 'src': src, 'dst': dst, 'edge_attr_128': edge_attr_128, 'edge_attr_64': edge_attr_64, 'L0_gnn_u': _L0_gnn_in['u'], 'L0_gnn_W1': _L0_gnn_in['W1'], 'L0_gnn_b1': _L0_gnn_in['b1'], 'L0_gnn_W2': _L0_gnn_in['W2'], 'L0_gnn_b2': _L0_gnn_in['b2'], 'L0_gnn_W3': _L0_gnn_in['W3'], 'L0_gnn_b3': _L0_gnn_in['b3'], 'L1_gnn_u': _L1_gnn_in['u'], 'L1_gnn_W1': _L1_gnn_in['W1'], 'L1_gnn_b1': _L1_gnn_in['b1'], 'L1_gnn_g1': _L1_gnn_in['g1'], 'L1_gnn_be1': _L1_gnn_in['be1'], 'L1_gnn_W2': _L1_gnn_in['W2'], 'L1_gnn_b2': _L1_gnn_in['b2'], 'L1_gnn_g2': _L1_gnn_in['g2'], 'L1_gnn_be2': _L1_gnn_in['be2'], 'L1_gnn_Wl': _L1_gnn_in['Wl'], 'L1_gnn_bl': _L1_gnn_in['bl']}

def reference(x, src, dst, edge_attr_128, edge_attr_64, L0_gnn_u, L0_gnn_W1, L0_gnn_b1, L0_gnn_W2, L0_gnn_b2, L0_gnn_W3, L0_gnn_b3, L1_gnn_u, L1_gnn_W1, L1_gnn_b1, L1_gnn_g1, L1_gnn_be1, L1_gnn_W2, L1_gnn_b2, L1_gnn_g2, L1_gnn_be2, L1_gnn_Wl, L1_gnn_bl):
    import jax
    import jax.numpy as jnp

    def _L0_gnn_ref(x, edge_index, edge_attr, u, batch, W1, b1, W2, b2, W3, b3):
        import jax, jax.numpy as jnp
        import numpy as np
        N = 50000
        E = 25000
        F = 128
        col = edge_index[1]
        n = x.shape[0]
        seg_sum = jax.ops.segment_sum(edge_attr, col, num_segments=n)
        counts = jax.ops.segment_sum(jnp.ones((edge_attr.shape[0],), edge_attr.dtype), col, num_segments=n)
        agg = seg_sum / jnp.maximum(counts, 1.0)[:, None]
        h = jnp.concatenate([x, agg], axis=-1)
        h = jax.nn.relu(h @ W1 + b1)
        h = jax.nn.relu(h @ W2 + b2)
        return h @ W3 + b3

    def _L1_gnn_ref(x, edge_index, edge_attr, u, batch, W1, b1, g1, be1, W2, b2, g2, be2, Wl, bl):
        import jax, jax.numpy as jnp
        import numpy as np
        N_NODES = 50000
        N_EDGES = 50000
        F_NODE = 128
        F_EDGE = 64
        L = 128
        EPS = 1e-05

        def _bn(h, gamma, beta):
            mu = jnp.mean(h, axis=0, keepdims=True)
            var = jnp.mean((h - mu) ** 2, axis=0, keepdims=True)
            return (h - mu) * jax.lax.rsqrt(var + EPS) * gamma + beta
        n = x.shape[0]
        row, col = (edge_index[0], edge_index[1])
        h = jnp.concatenate([x[row], edge_attr], axis=1)
        h = jax.nn.relu(_bn(h @ W1 + b1, g1, be1))
        s = jax.ops.segment_sum(h, col, num_segments=n)
        cnt = jax.ops.segment_sum(jnp.ones((h.shape[0], 1), h.dtype), col, num_segments=n)
        agg = jnp.where(cnt > 0, s / jnp.maximum(cnt, 1.0), 0.0)
        h2 = jnp.concatenate([x, agg], axis=1)
        h2 = jax.nn.relu(_bn(h2 @ W2 + b2, g2, be2))
        return jax.nn.relu(h2 @ Wl + bl)
    edge_index = jnp.stack([src, dst])
    batch0 = jnp.zeros((50000,), jnp.int32)
    x = _layernorm(x + _L0_gnn_ref(x, edge_index, edge_attr_128, L0_gnn_u, batch0, L0_gnn_W1, L0_gnn_b1, L0_gnn_W2, L0_gnn_b2, L0_gnn_W3, L0_gnn_b3), axis=-1)
    x = _layernorm(x + _L1_gnn_ref(x, edge_index, edge_attr_64, L1_gnn_u, batch0, L1_gnn_W1, L1_gnn_b1, L1_gnn_g1, L1_gnn_be1, L1_gnn_W2, L1_gnn_b2, L1_gnn_g2, L1_gnn_be2, L1_gnn_Wl, L1_gnn_bl), axis=-1)
    return x

_drawn_inputs = setup_inputs


def setup_inputs(seed=0):
    import zlib

    import numpy as np

    out = dict(_drawn_inputs(seed))
    spreads = {'L1_gnn_b1': (0.0, 0.8),
     'L1_gnn_g1': (1.0, 0.2),
     'L1_gnn_be1': (0.0, 0.495),
     'L1_gnn_b2': (0.0, 0.8),
     'L1_gnn_g2': (1.0, 0.2),
     'L1_gnn_be2': (0.0, 0.1),
     'L1_gnn_bl': (0.0, 0.1)}
    factors = {'L0_gnn_b1': 8.0, 'L0_gnn_b2': 3.201}
    for name, (base, spread) in spreads.items():
        noise = np.random.default_rng([zlib.crc32(name.encode()), seed]).standard_normal(out[name].shape)
        drawn = base * np.exp(spread * noise) if base else spread * noise
        out[name] = jnp.asarray(drawn.astype(out[name].dtype))
    for name, factor in factors.items():
        out[name] = (out[name] * factor).astype(out[name].dtype)
    return out
```

```python
from contextlib import ExitStack

import concourse.bass as bass
from concourse import mybir

F32 = mybir.dt.float32
BF16 = mybir.dt.bfloat16
F16 = mybir.dt.float16
I32 = mybir.dt.int32
ALU = mybir.AluOpType
ACT = mybir.ActivationFunctionType
AX_X = mybir.AxisListType.X

P = 128
F = 128
FE = 64
N = 50000
E = 50000
ROWS = 4
G = P * ROWS
NG = -(-N // G)
NPAD = NG * G
LAST = (N - (NG - 1) * G) // ROWS
WIN = 128
NW = G // WIN
TPC = 2
CHUNK = TPC * P
TABW = 512
TILES = -(-E // P)
BIG = 1.0e9
EXTRA = E + (TILES * P - E)
DSCR = EXTRA + 2 * CHUNK
TAB_START, TAB_LOOPS, TAB_BEFORE, TAB_ANY = 0, TABW, 2 * TABW, 3 * TABW
TAB = 3 * TABW + P
EPS = 1e-5
PAIRS = NG // 2

assert NG % 2 == 0 and (N - (NG - 1) * G) % ROWS == 0 and E == N


def after(eng, sem, count, apart=False):
    if not isinstance(count, int) or count > 0:
        if apart and not isinstance(count, int):
            eng.wait_ge(sem, 1)
        eng.wait_ge(sem, count)


def steps(eng, body, stages, ahead=2, behind=0):
    def pair(u):
        for s in range(2):
            i = 2 * u + s if isinstance(u, int) else None
            body(u, s, [True if i is None else 0 <= i - k < NG for k in range(stages)])
    for u in range(ahead):
        pair(u)
    with eng.Fori(ahead, PAIRS - behind) as u:
        pair(u)
    for u in range(PAIRS - behind, PAIRS + stages // 2):
        pair(u)


class Windows:

    def __init__(self, nc, ctx, tag, tab, const):
        def sb(name, shape, dt):
            return ctx.enter_context(nc.sbuf_tensor(f"{tag}_{name}", shape, dt))

        def sem(name):
            return ctx.enter_context(nc.semaphore(f"{tag}_{name}"))

        self.tab, self.const = tab, const
        two = range(2)
        self.rows = [sb(f"rows{s}", [P, NW, TPC * F], F32) for s in two]
        self.dst = [sb(f"dst{s}", [P, NW, TPC], F32) for s in two]
        self.rest = [sb(f"rest{s}", [P, NW, TPC * F], F32) for s in two]
        self.low = [sb(f"low{s}", [P, NW, TPC, F + 2], BF16) for s in two]
        self.hot = [sb(f"hot{s}", [P, NW, TPC, WIN], BF16) for s in two]
        self.xrows = [sb(f"xrows{s}", [P, TPC * F], F32) for s in two]
        self.xdst = [sb(f"xdst{s}", [P, TPC], F32) for s in two]
        self.xrest = [sb(f"xrest{s}", [P, TPC * F], F32) for s in two]
        self.xlow = [sb(f"xlow{s}", [P, TPC, F + 2], BF16) for s in two]
        self.xhot = [sb(f"xhot{s}", [P, TPC, WIN], BF16) for s in two]
        self.count = sb("count", [P, NW], F32)
        self.inv = sb("inv", [P, NW], F32)
        self.mean = sb("mean", [P, NW, F], F32)
        self.sums = [ctx.enter_context(nc.psum_tensor(f"{tag}_sums{b}", [P, 2, F + 1], F32)) for b in two]
        self.rows_in = [sem(f"rows_in{s}") for s in two]
        self.xrows_in = [sem(f"xrows_in{s}") for s in two]
        self.rest_done = sem("rest_done")
        self.split_done = sem("split_done")
        self.xrest_done = sem("xrest_done")
        self.xsplit_done = [sem(f"xsplit_done{s}") for s in two]
        self.hot_done = sem("hot_done")
        self.xhot_done = [sem(f"xhot_done{s}") for s in two]
        self.sums_done = sem("sums_done")
        self.xsums_done = [sem(f"xsums_done{s}") for s in two]
        self.count_done = sem("count_done")
        self.inv_done = sem("inv_done")
        self.mean_done = sem("mean_done")
        self.ones_done = sem("ones_done")

    def further(self, nc, eng, g, body):
        tab = self.tab
        some = eng.value_load(tab[0:1, bass.ds(g + TAB_ANY, 1)], min_val=0, max_val=1 << 20)
        with eng.If(some > 0):
            for j in range(NW):
                w = g * NW + j
                loops = eng.value_load(tab[0:1, bass.ds(w + TAB_LOOPS, 1)], min_val=0, max_val=1 << 20)
                before = eng.value_load(tab[0:1, bass.ds(w + TAB_BEFORE, 1)], min_val=0, max_val=1 << 20)
                with eng.If(loops > 0):
                    with eng.Fori(0, loops) as t:
                        body(j, t, before + t)
                    eng.nop()
                eng.nop()
            eng.nop()

    def load(self, nc, sp, u, s, src, dscr):
        g = 2 * u + s
        after(sp, self.sums_done, g - 1, apart=True)
        for j in range(NW):
            start = sp.value_load(self.tab[0:1, bass.ds(g * NW + (TAB_START + j), 1)], min_val=0, max_val=E - CHUNK)
            sp.dma_start(self.rows[s][:, j, :],
                         src[bass.ds(start, CHUNK), :].rearrange("(p t) f -> p (t f)", t=TPC)).then_inc(self.rows_in[s], 16)
            sp.dma_start(self.dst[s][:, j, :],
                         dscr[bass.ds(start, CHUNK), :].rearrange("(p t) o -> p (t o)", t=TPC)).then_inc(self.rows_in[s], 16)

    def load_further(self, nc, sp, g, src, dscr):
        def body(j, t, turn):
            start = sp.value_load(self.tab[0:1, bass.ds(g * NW + (TAB_START + j), 1)], min_val=0, max_val=E - CHUNK)
            for s in range(2):
                after(sp, self.xsums_done[s], turn + 1, apart=True)
                pos = sp.snap(start + t * (2 * CHUNK) + (1 + s) * CHUNK)
                with sp.If(pos > E - CHUNK):
                    sp.dma_start(self.xrows[s][:, :],
                                 src[E - CHUNK:E, :].rearrange("(p t) f -> p (t f)", t=TPC)).then_inc(self.xrows_in[s], 16)
                    shift = EXTRA - (E // CHUNK) * CHUNK
                    far = (pos + shift).with_bounds(min_val=0, max_val=DSCR - CHUNK)
                    sp.dma_start(self.xdst[s][:, :],
                                 dscr[bass.ds(far, CHUNK), :].rearrange("(p t) o -> p (t o)", t=TPC)).then_inc(self.xrows_in[s], 16)
                with sp.Else():
                    near = (pos + 0).with_bounds(min_val=0, max_val=E - CHUNK)
                    sp.dma_start(self.xrows[s][:, :],
                                 src[bass.ds(near, CHUNK), :].rearrange("(p t) f -> p (t f)", t=TPC)).then_inc(self.xrows_in[s], 16)
                    sp.dma_start(self.xdst[s][:, :],
                                 dscr[bass.ds(near, CHUNK), :].rearrange("(p t) o -> p (t o)", t=TPC)).then_inc(self.xrows_in[s], 16)
                sp.nop()
        self.further(nc, sp, g, body)

    def ones(self, nc, pool):
        for s in range(2):
            nc.gpsimd.memset(self.low[s][:, :, :, F:F + 2], 1.0).then_inc(self.ones_done, 1)
            nc.gpsimd.memset(self.xlow[s][:, :, F:F + 2], 1.0).then_inc(self.ones_done, 1)

    def split(self, nc, pool, u, s):
        g = 2 * u + s
        pool.wait_ge(self.rows_in[s], (u + 1) * (16 * 2 * NW))
        rows, rest = self.rows[s][:, :, :], self.rest[s][:, :, :]
        nc.gpsimd.tensor_tensor(rest, rows, upper(rows), ALU.subtract).then_inc(self.rest_done, 1)
        pool.wait_ge(self.rest_done, g + 1)
        nc.gpsimd.tensor_tensor(self.low[s][:, :, :, 0:F], self.rest[s][:, :, :].rearrange("p j (t f) -> p j t f", t=TPC),
                                upper(rest).rearrange("p j (t f) -> p j t f", t=TPC),
                                ALU.subtract).then_inc(self.split_done, 1)

    def split_further(self, nc, pool, g):
        def body(j, t, turn):
            for s in range(2):
                pool.wait_ge(self.xrows_in[s], (turn + 1) * 32)
                rows, rest = self.xrows[s][:, :], self.xrest[s][:, :]
                nc.gpsimd.tensor_tensor(rest, rows, upper(rows), ALU.subtract).then_inc(self.xrest_done, 1)
                pool.wait_ge(self.xrest_done, turn * 2 + (s + 1))
                nc.gpsimd.tensor_tensor(self.xlow[s][:, :, 0:F], rest.rearrange("p (t f) -> p t f", t=TPC),
                                        upper(rest).rearrange("p (t f) -> p t f", t=TPC),
                                        ALU.subtract).then_inc(self.xsplit_done[s], 1)
        self.further(nc, pool, g, body)

    def hots(self, nc, dve, u, s, g):
        dve.wait_ge(self.rows_in[s], (u + 1) * (16 * 2 * NW))
        for j in range(NW):
            for t in range(TPC):
                op = nc.vector.tensor_scalar(self.hot[s][:, j, t, :], self.const.node[:, j, :], self.dst[s][:, j, t:t + 1],
                                             self.const.minus_first[:, bass.ds(g, 1)], ALU.subtract, ALU.is_equal)
        op.then_inc(self.hot_done, 1)

    def hots_further(self, nc, dve, g):
        def body(j, t, turn):
            for s in range(2):
                dve.wait_ge(self.xrows_in[s], (turn + 1) * 32)
                for k in range(TPC):
                    op = nc.vector.tensor_scalar(self.xhot[s][:, k, :], self.const.node[:, j, :], self.xdst[s][:, k:k + 1],
                                                 self.const.minus_first[:, bass.ds(g, 1)], ALU.subtract, ALU.is_equal)
                op.then_inc(self.xhot_done[s], 1)
        self.further(nc, dve, g, body)

    def sum_tile(self, nc, out, hot, rows, rest, low, start, stop, further=False):
        nc.tensor.matmul(out, hot, low, start=start, stop=False, skip_group_check=further)
        nc.tensor.matmul(out[:, 0:F], hot, rows, start=False, stop=False, skip_group_check=further)
        return nc.tensor.matmul(out[:, 0:F], hot, rest, start=False, stop=stop, skip_group_check=further)

    def sum_windows(self, nc, pe, u, s, g, half):
        if half == 0:
            pe.wait_ge(self.hot_done, g + 1)
            pe.wait_ge(self.split_done, g + 1)
            after(pe, self.mean_done, g)
        for j in (2 * half, 2 * half + 1):
            for t in range(TPC):
                last = half == 1 and j == NW - 1 and t == TPC - 1
                if last:
                    self.sum_further(nc, pe, g)
                mm = self.sum_tile(nc, self.sums[half][:, j % 2, :], self.hot[s][:, j, t, :],
                                   upper(self.rows[s][:, j, t * F:(t + 1) * F]), upper(self.rest[s][:, j, t * F:(t + 1) * F]),
                                   self.low[s][:, j, t, 0:F + 1], start=(j % 2 == 0 and t == 0),
                                   stop=(j % 2 == 1 and t == TPC - 1))
        if half == 1:
            mm.then_inc(self.sums_done, 1)

    def sum_further(self, nc, pe, g):
        def body(j, t, turn):
            for s in range(2):
                pe.wait_ge(self.xhot_done[s], turn + 1)
                pe.wait_ge(self.xsplit_done[s], turn + 1)
                for k in range(TPC):
                    mm = self.sum_tile(nc, self.sums[j // 2][:, j % 2, :], self.xhot[s][:, k, :],
                                       upper(self.xrows[s][:, k * F:(k + 1) * F]), upper(self.xrest[s][:, k * F:(k + 1) * F]),
                                       self.xlow[s][:, k, 0:F + 1], start=False, stop=False, further=True)
                mm.then_inc(self.xsums_done[s], 1)
        self.further(nc, pe, g, body)

    def means(self, nc, dve, g, mean_read):
        dve.wait_ge(self.sums_done, g + 1)
        for b in range(2):
            op = nc.vector.tensor_scalar(self.count[:, 2 * b:2 * b + 2], self.sums[b][:, :, F], 1.0, None, ALU.max)
        op.then_inc(self.count_done, 1)
        dve.wait_ge(self.count_done, g + 1)
        nc.vector.reciprocal(self.inv[:, :], self.count[:, :]).then_inc(self.inv_done, 1)
        dve.wait_ge(self.inv_done, g + 1)
        after(dve, mean_read, g)
        for b in range(2):
            op = nc.vector.tensor_tensor(self.mean[:, 2 * b:2 * b + 2, :], self.sums[b][:, :, 0:F],
                                         self.inv[:, 2 * b:2 * b + 2].unsqueeze(2).to_broadcast([P, 2, F]), ALU.mult)
        op.then_inc(self.mean_done, 1)


def upper(ap):
    v = ap.bitcast(BF16)
    if len(v.shape) == 2:
        return v[:, 1::2]
    return v[:, :, 1::2]


class Constants:
    pass


def rows_of(dram, g, width, parts=P):
    if isinstance(g, int):
        view = dram[g * G:g * G + parts * ROWS, :]
    else:
        view = dram[bass.ds(g * G, parts * ROWS), :]
    return view.rearrange("(p k) f -> p (k f)", k=ROWS)


def window_order(ap):
    return ap.rearrange("f (j k q) -> f k j q", j=NW, k=ROWS)


def prepare(nc, ctx, A, S, const, tab):
    with ExitStack() as own:
        def sb(name, shape, dt):
            return own.enter_context(nc.sbuf_tensor(f"t_{name}", shape, dt))

        def sem(name):
            return own.enter_context(nc.semaphore(f"t_{name}"))

        DP = 125
        DR = E // DP
        C8 = 2 * TABW // P
        CW = TABW // P
        d0 = sb("d0", [DP, DR], I32)
        d1 = sb("d1", [DP, DR], I32)
        f0 = sb("f0", [DP, DR], F32)
        f1 = sb("f1", [DP, DR], F32)
        down = sb("down", [DP, DR], F32)
        falls = sb("falls", [P, 1], F32)
        unsorted = sb("unsorted", [P, 1], F32)
        sorted_ = sb("sorted", [P, 1], F32)
        heads_i = sb("heads_i", [1, TILES], I32)
        heads = sb("heads", [1, TILES], F32)
        heads_all = sb("heads_all", [P, TILES], F32)
        below = sb("below", [P, TILES], F32)
        ones = sb("ones", [P, P], F32)
        thr_i = sb("thr_i", [P, C8], I32)
        thr = sb("thr", [P, C8], F32)
        whole = sb("whole", [P, C8], F32)
        row = sb("row", [P, C8], F32)
        row_i = sb("row_i", [P, C8], I32)
        tile = sb("tile", [P, C8, P], F32)
        under = sb("under", [P, C8, P], F32)
        part = sb("part", [P, C8], F32)
        pos = sb("pos", [P, C8], F32)
        size = sb("size", [P, CW], F32)
        size_i = sb("size_i", [P, CW], I32)
        loops_i = sb("loops_i", [P, CW], I32)
        loops = sb("loops", [P, CW], F32)
        start = sb("start", [P, CW], F32)
        start_i = sb("start_i", [P, CW], I32)
        far = sb("far", [1, DSCR - E], F32)
        tail_i = sb("tail_i", [1, E % CHUNK], I32)
        line = sb("line", [1, 2, TABW], I32)
        run = [sb(f"run{k}", [1, TABW], F32) for k in range(2)]
        lone = sb("lone", [1, TABW], F32)
        node_i = sb("node_i", [P, NW, WIN], I32)
        first_i = sb("first_i", [P, NG], I32)
        ps_falls = own.enter_context(nc.psum_tensor("t_ps_falls", [P, 1], F32))
        ps_heads = own.enter_context(nc.psum_tensor("t_ps_heads", [P, TILES], F32))

        loaded = sem("loaded")
        weights_in = sem("weights_in")
        filled = sem("filled")
        made = sem("made")
        heads_done = sem("heads_done")
        spread = sem("spread")
        written = sem("written")
        rows_done = sem("rows_done")
        gathered = sem("gathered")
        found = sem("found")
        tables_out = sem("tables_out")
        tables_in = sem("tables_in")
        v = sem("v")
        block = own.enter_context(nc.Block())

        @block.sync
        def _(sp):
            dst = A["dst"]
            sp.dma_start(d0[:, :], dst.rearrange("(p r) -> p r", p=DP)).then_inc(loaded, 16)
            sp.dma_start(heads_i[:, 0:TILES - 1],
                         dst[0:(TILES - 1) * P].rearrange("(o i s) -> o i s", o=1, s=P)[:, :, 0]).then_inc(loaded, 16)
            sp.dma_start(heads_i[:, TILES - 1:TILES],
                         dst[(TILES - 1) * P:(TILES - 1) * P + 1].rearrange("(o i) -> o i", o=1)).then_inc(loaded, 16)
            sp.dma_start(tail_i[:, :], dst[E - E % CHUNK:E].rearrange("(o i) -> o i", o=1)).then_inc(loaded, 16)
            sp.dma_start(d1[0:DP - 1, :], dst[1:1 + (DP - 1) * DR].rearrange("(p r) -> p r", r=DR)).then_inc(loaded, 16)
            sp.dma_start(d1[DP - 1:DP, 0:DR - 1], dst[1 + (DP - 1) * DR:E].rearrange("(o r) -> o r", o=1)).then_inc(loaded, 16)
            sp.dma_start(d1[DP - 1:DP, DR - 1:DR], dst[E - 1:E].rearrange("(o r) -> o r", o=1)).then_inc(loaded, 16)
            for to, what in const.loads:
                sp.dma_start(to, what).then_inc(weights_in, 16)
            sp.wait_ge(made, 1)
            sp.dma_start(S["dscr"][0:E, :].rearrange("(p r) o -> p (r o)", p=DP), f0[:, :]).then_inc(written, 16)
            sp.dma_start(S["dscr"][E:DSCR, :].rearrange("(q r) o -> q (r o)", q=1), far[:, :]).then_inc(written, 16)
            sp.wait_ge(found, 1)
            sp.dma_start(S["tabs"][0:1, :].rearrange("o (c p) -> p (o c)", p=P), start_i[:, :]).then_inc(tables_out, 16)
            sp.dma_start(S["tabs"][1:2, :].rearrange("o (c p) -> p (o c)", p=P), loops_i[:, :]).then_inc(tables_out, 16)
            sp.wait_ge(tables_out, 32)
            sp.dma_start(line[:, :, :], S["tabs"].rearrange("(o t) w -> o t w", o=1)).then_inc(tables_in, 16)
            sp.wait_ge(weights_in, 16 * len(const.loads))

        @block.gpsimd
        def _(pool):
            nc.gpsimd.iota(node_i[:, :, :].rearrange("p j (k q) -> p j k q", k=ROWS),
                           [[WIN, NW], [1, ROWS], [ROWS, WIN // ROWS]], base=0, channel_multiplier=0).then_inc(filled, 1)
            nc.gpsimd.iota(first_i[:, :], [[-G, NG]], base=0, channel_multiplier=0).then_inc(filled, 1)
            nc.gpsimd.iota(thr_i[:, 0:CW], [[P * WIN, CW]], base=0, channel_multiplier=WIN).then_inc(filled, 1)
            nc.gpsimd.iota(thr_i[:, CW:C8], [[P * WIN, CW]], base=WIN, channel_multiplier=WIN).then_inc(filled, 1)
            nc.gpsimd.memset(ones[:, :], 1.0).then_inc(filled, 1)
            nc.gpsimd.memset(const.ident[:, :], 0.0).then_inc(filled, 1)
            pool.wait_ge(filled, 6)
            nc.gpsimd.affine_select(out=const.ident[:, :], in_=const.ident[:, :], compare_op=ALU.not_equal, fill=1.0,
                                    base=0, pattern=[[-1, P]], channel_multiplier=1).then_inc(filled, 1)
            pool.wait_ge(written, 32)
            pool.wait_ge(rows_done, 1)
            for c in range(C8):
                nc.gpsimd.indirect_dma_start(
                    out=tile[:, c, :], out_offset=None,
                    in_=S["dscr"][0:TILES * P, :].rearrange("(i s) o -> i (s o)", s=P),
                    in_offset=bass.IndirectOffsetOnAxis(ap=row_i[:, c:c + 1], axis=0),
                    bounds_check=TILES - 1, oob_is_err=True).then_inc(gathered, 16)
            pool.wait_ge(gathered, 16 * C8)

        @block.tensor
        def _(pe):
            pe.wait_ge(filled, 6)
            pe.wait_ge(heads_done, 1)
            nc.tensor.matmul(ps_heads[:, :], ones[0:1, :], heads[:, :], start=True, stop=True).then_inc(spread, 1)
            pe.wait_ge(heads_done, 2)
            nc.tensor.matmul(ps_falls[:, :], ones[0:DP, :], falls[0:DP, :], start=True, stop=True).then_inc(spread, 1)

        @block.vector
        def _(dve):
            n = [0]

            def then(op):
                n[0] += 1
                op.then_inc(v, 1)
                dve.wait_ge(v, n[0])

            dve.wait_ge(loaded, 16 * 7)
            nc.vector.tensor_copy(heads[:, :], heads_i[:, :]).then_inc(heads_done, 1)
            then(nc.vector.memset(far[:, :], BIG))
            then(nc.vector.tensor_copy(far[:, EXTRA - E + CHUNK - E % CHUNK:EXTRA - E + CHUNK], tail_i[:, :]))
            nc.vector.tensor_copy(f1[:, :], d1[:, :])
            then(nc.vector.tensor_copy(f0[:, :], d0[:, :]))
            nc.vector.tensor_tensor(down[:, :], f0[:, :], f1[:, :], ALU.is_gt).then_inc(made, 1)
            dve.wait_ge(made, 1)
            nc.vector.tensor_reduce(falls[0:DP, :], down[:, :], AX_X, ALU.add).then_inc(heads_done, 1)
            dve.wait_ge(filled, 7)
            nc.vector.tensor_copy(const.node[:, :, :], node_i[:, :, :])
            nc.vector.tensor_copy(const.minus_first[:, :], first_i[:, :])
            nc.vector.tensor_copy(thr[:, :], thr_i[:, :])
            dve.wait_ge(spread, 2)
            nc.vector.tensor_scalar(unsorted[:, :], ps_falls[:, :], 0.5, None, ALU.is_gt)
            nc.vector.tensor_scalar(sorted_[:, :], ps_falls[:, :], 0.5, None, ALU.is_lt)
            then(nc.vector.tensor_copy(heads_all[:, :], ps_heads[:, :]))
            for c in range(C8):
                then(nc.vector.tensor_scalar(below[:, :], heads_all[:, :], thr[:, c:c + 1], None, ALU.is_lt))
                then(nc.vector.tensor_reduce(whole[:, c:c + 1], below[:, :], AX_X, ALU.add))
            then(nc.vector.tensor_scalar(row[:, :], whole[:, :], -1.0, 0.0, ALU.add, ALU.max))
            nc.vector.tensor_copy(row_i[:, :], row[:, :]).then_inc(rows_done, 1)
            dve.wait_ge(gathered, 16 * C8)
            for c in range(C8):
                then(nc.vector.tensor_scalar(under[:, c, :], tile[:, c, :], thr[:, c:c + 1], None, ALU.is_lt))
            then(nc.vector.tensor_reduce(part[:, :], under[:, :, :], AX_X, ALU.add))
            then(nc.vector.scalar_tensor_tensor(out=pos[:, :], in0=row[:, :], scalar=float(P), in1=part[:, :],
                                                op0=ALU.mult, op1=ALU.add))
            then(nc.vector.tensor_scalar(pos[:, :], pos[:, :], sorted_[:, 0:1], None, ALU.mult))
            then(nc.vector.tensor_scalar(whole[:, 0:1], unsorted[:, :], float(E), None, ALU.mult))
            then(nc.vector.tensor_scalar(pos[:, CW:C8], pos[:, CW:C8], whole[:, 0:1], None, ALU.add))
            then(nc.vector.tensor_tensor(size[:, :], pos[:, CW:C8], pos[:, 0:CW], ALU.subtract))
            then(nc.vector.tensor_scalar(size[:, :], size[:, :], float(-CHUNK), 0.0, ALU.add, ALU.max))
            then(nc.vector.tensor_scalar(size[:, :], size[:, :], float(2 * CHUNK - 1), None, ALU.add))
            then(nc.vector.tensor_copy(size_i[:, :], size[:, :]))
            then(nc.vector.tensor_scalar(loops_i[:, :], size_i[:, :], (2 * CHUNK).bit_length() - 1, None, ALU.logical_shift_right))
            then(nc.vector.tensor_copy(loops[:, :], loops_i[:, :]))
            then(nc.vector.tensor_scalar(loops[:, :], loops[:, :], float(-2 * CHUNK), float(E - CHUNK), ALU.mult, ALU.add))
            then(nc.vector.tensor_tensor(start[:, :], pos[:, 0:CW], loops[:, :], ALU.min))
            then(nc.vector.tensor_scalar(start[:, :], start[:, :], 0.0, None, ALU.max))
            nc.vector.tensor_copy(start_i[:, :], start[:, :]).then_inc(found, 1)
            dve.wait_ge(tables_in, 16)
            then(nc.vector.tensor_copy(tab[:, TAB_START:TAB_START + TABW], line[:, 0, :]))
            then(nc.vector.tensor_copy(tab[:, TAB_LOOPS:TAB_LOOPS + TABW], line[:, 1, :]))
            then(nc.vector.tensor_copy(lone[:, :], line[:, 1, :]))
            then(nc.vector.tensor_copy(run[0][:, :], line[:, 1, :]))
            reach, k = 1, 0
            while reach < TABW:
                then(nc.vector.tensor_copy(run[1 - k][:, 0:reach], run[k][:, 0:reach]))
                then(nc.vector.tensor_tensor(run[1 - k][:, reach:TABW], run[k][:, reach:TABW],
                                             run[k][:, 0:TABW - reach], ALU.add))
                reach, k = 2 * reach, 1 - k
            then(nc.vector.tensor_tensor(run[1 - k][:, :], run[k][:, :], lone[:, :], ALU.subtract))
            then(nc.vector.tensor_copy(tab[:, TAB_BEFORE:TAB_BEFORE + TABW], run[1 - k][:, :]))
            then(nc.vector.tensor_reduce(run[k][:, 0:P], lone[:, :].rearrange("o (g j) -> o g j", j=NW), AX_X, ALU.add))
            then(nc.vector.tensor_copy(tab[:, TAB_ANY:TAB_ANY + P], run[k][:, 0:P]))


def layernorm_stats(nc, dve, rows, stats, moments, stats_done, moments_done, g):
    for k in range(ROWS):
        op = nc.vector.bn_stats(stats[:, k, :], rows[:, k, :])
    op.then_inc(stats_done, 1)
    after(dve, stats_done, g + 1, apart=True)
    for k in range(ROWS):
        op = nc.vector.bn_aggr(moments[:, k, :], stats[:, k, :])
    op.then_inc(moments_done, 1)


def layer0(nc, ctx, A, S, const, tab):
    with ExitStack() as own:
        def sb(name, shape, dt=F32):
            return own.enter_context(nc.sbuf_tensor(f"a_{name}", shape, dt))

        def psum(name):
            return own.enter_context(nc.psum_tensor(f"a_{name}", [P, G], F32))

        def sem(name):
            return own.enter_context(nc.semaphore(f"a_{name}"))

        win = Windows(nc, own, "a", tab, const)
        x = [sb(f"x{s}", [P, ROWS * F]) for s in range(2)]
        xT = [sb(f"xT{s}", [P, G]) for s in range(2)]
        meanT = sb("meanT", [P, G])
        h1 = sb("h1", [P, G])
        h2 = sb("h2", [P, G])
        sumT = sb("sumT", [P, G])
        stats = sb("stats", [P, ROWS, 6])
        moments = sb("moments", [P, ROWS, 2])
        std = sb("std", [P, ROWS])
        rstd = sb("rstd", [P, ROWS])
        shift = sb("shift", [P, ROWS])
        out = [sb(f"out{s}", [P, ROWS * F]) for s in range(2)]
        ps_x, ps_mean, ps_h1, ps_h2, ps_o, ps_r = (psum(k) for k in ("ps_x", "ps_mean", "ps_h1", "ps_h2", "ps_o", "ps_r"))

        x_in = [sem(f"x_in{s}") for s in range(2)]
        x_turned, mean_turned, xT_done, meanT_done = (sem(k) for k in ("x_turned", "mean_turned", "xT_done", "meanT_done"))
        mm1, h1_done, mm2, h2_done, mm3, sumT_done = (sem(k) for k in ("mm1", "h1_done", "mm2", "h2_done", "mm3", "sumT_done"))
        sum_turned, stats_done, moments_done, std_done, rstd_done, shift_done, out_done = (
            sem(k) for k in ("sum_turned", "stats_done", "moments_done", "std_done", "rstd_done", "shift_done", "out_done"))
        stored = [sem(f"stored{s}") for s in range(2)]
        block = own.enter_context(nc.Block())

        @block.sync
        def _(sp):
            def step(u, s, parts=P):
                g = 2 * u + s
                win.load(nc, sp, u, s, A["edge_attr_128"], S["dscr"])
                after(sp, x_turned, g - 1)
                sp.dma_start(x[s][0:parts, :], rows_of(A["x"], g, F, parts)).then_inc(x_in[s], 16)
                if not isinstance(g, int) or g > 0:
                    win.load_further(nc, sp, g - 1, A["edge_attr_128"], S["dscr"])

            for u in range(2):
                step(u, 0)
                step(u, 1)
            with sp.Fori(2, PAIRS - 1) as u:
                step(u, 0)
                step(u, 1)
            step(PAIRS - 1, 0)
            step(PAIRS - 1, 1, LAST)
            win.load_further(nc, sp, NG - 1, A["edge_attr_128"], S["dscr"])

        @block.gpsimd
        def _(pool):
            win.ones(nc, pool)

            def step(u, s, valid):
                win.split(nc, pool, u, s)
                win.split_further(nc, pool, 2 * u + s)
            steps(pool, step, 1)

        @block.tensor
        def _(pe):
            pe.wait_ge(win.ones_done, 4)
            for s in range(2):
                pe.sem_inc(win.xsums_done[s], 1)

            def step(u, s, valid):
                g = 2 * u + s
                now, lag1, lag2 = valid
                if lag2:
                    pe.wait_ge(sumT_done, g - 1)
                    after(pe, out_done, g - 2)
                    for k in range(ROWS):
                        mm = nc.tensor.transpose(ps_r[:, k * P:(k + 1) * P], sumT[:, k * P:(k + 1) * P], const.ident[:, :])
                    mm.then_inc(sum_turned, 1)
                if lag1:
                    pe.wait_ge(xT_done, g)
                    after(pe, h1_done, g - 1)
                    nc.tensor.matmul(ps_h1[:, :], const.w1[:, 0, :], xT[1 - s][:, :], start=True, stop=False)
                    pe.wait_ge(meanT_done, g)
                    nc.tensor.matmul(ps_h1[:, :], const.w1[:, 1, :], meanT[:, :], start=False, stop=True).then_inc(mm1, 1)
                if now:
                    win.sum_windows(nc, pe, u, s, g, 0)
                if lag1:
                    pe.wait_ge(h1_done, g)
                    after(pe, h2_done, g - 1)
                    nc.tensor.matmul(ps_h2[:, :], const.w2[:, :], h1[:, :], start=True, stop=True).then_inc(mm2, 1)
                if now:
                    win.sum_windows(nc, pe, u, s, g, 1)
                if lag1:
                    pe.wait_ge(h2_done, g)
                    after(pe, sumT_done, g - 1)
                    nc.tensor.matmul(ps_o[:, :], const.w3[:, :], h2[:, :], start=True, stop=True).then_inc(mm3, 1)
                if now:
                    pe.wait_ge(x_in[s], (u + 1) * 16)
                    after(pe, xT_done, g)
                    for k in range(ROWS):
                        mm = nc.tensor.transpose(ps_x[:, k * P:(k + 1) * P], x[s][:, k * F:(k + 1) * F], const.ident[:, :])
                    mm.then_inc(x_turned, 1)
                    pe.wait_ge(win.mean_done, g + 1)
                    after(pe, meanT_done, g)
                    for j in range(NW):
                        mm = nc.tensor.transpose(ps_mean[:, j * P:(j + 1) * P], win.mean[:, j, :], const.ident[:, :])
                    mm.then_inc(mean_turned, 1)
            steps(pe, step, 3)

        @block.scalar
        def _(act):
            def store(u, s):
                g = 2 * u + s
                act.wait_ge(out_done, g)
                act.dma_start(rows_of(S["x1"], g - 1, F), out[1 - s][:, :]).then_inc(stored[1 - s], 16)

            def step(u, s, valid):
                g = 2 * u + s
                now, lag1, lag2 = valid
                if lag1:
                    act.wait_ge(mm1, g)
                    after(act, mm2, g - 1)
                    nc.scalar.activation(h1[:, :], ps_h1[:, :], ACT.Relu, bias=const.b1[:, 0:1], scale=1.0).then_inc(h1_done, 1)
                if lag2:
                    act.wait_ge(moments_done, g - 1)
                    nc.scalar.activation(std[:, :], moments[:, :, 1], ACT.Sqrt, bias=const.eps[:, 0:1], scale=1.0).then_inc(std_done, 1)
                if lag1:
                    act.wait_ge(mm2, g)
                    after(act, mm3, g - 1)
                    nc.scalar.activation(h2[:, :], ps_h2[:, :], ACT.Relu, bias=const.b2[:, 0:1], scale=1.0).then_inc(h2_done, 1)
                if lag2:
                    act.wait_ge(shift_done, g - 1)
                    after(act, stored[s], (u - 1) * 16)
                    for k in range(ROWS):
                        op = nc.scalar.activation(out[s][:, k * F:(k + 1) * F], ps_r[:, k * F:(k + 1) * F], ACT.Identity,
                                                  bias=shift[:, k:k + 1], scale=rstd[:, k:k + 1])
                    op.then_inc(out_done, 1)
                    act.wait_ge(out_done, g - 1)
                    act.dma_start(rows_of(S["x1"], g - 2, F), out[s][:, :]).then_inc(stored[s], 16)
                if now:
                    act.wait_ge(x_turned, g + 1)
                    after(act, sumT_done, g - 1)
                    nc.scalar.activation(xT[s][:, :], ps_x[:, :], ACT.Identity).then_inc(xT_done, 1)
                    act.wait_ge(mean_turned, g + 1)
                    after(act, mm1, g)
                    nc.scalar.activation(meanT[:, :].rearrange("f (k j q) -> f k j q", k=ROWS, j=NW), window_order(ps_mean[:, :]),
                                         ACT.Identity).then_inc(meanT_done, 1)
            steps(act, step, 3)
            for s in range(2):
                act.wait_ge(stored[s], 16 * PAIRS)

        @block.vector
        def _(dve):
            win.hots(nc, dve, 0, 0, 0)

            def step(u, s, valid):
                g = 2 * u + s
                now, lag1, lag2 = valid
                if lag2:
                    dve.wait_ge(sum_turned, g - 1)
                    layernorm_stats(nc, dve, ps_r[:, :].rearrange("p (k f) -> p k f", k=ROWS), stats, moments,
                                    stats_done, moments_done, g - 2)
                if now and not (isinstance(u, int) and g + 1 >= NG):
                    win_next(u, s)
                if lag2:
                    dve.wait_ge(std_done, g - 1)
                    nc.vector.reciprocal(rstd[:, :], std[:, :]).then_inc(rstd_done, 1)
                    dve.wait_ge(rstd_done, g - 1)
                    nc.vector.scalar_tensor_tensor(out=shift[:, :], in0=moments[:, :, 0], scalar=-1.0, in1=rstd[:, :],
                                                   op0=ALU.mult, op1=ALU.mult).then_inc(shift_done, 1)
                if now:
                    win.hots_further(nc, dve, g)
                    win.means(nc, dve, g, mean_turned)
                if lag1:
                    dve.wait_ge(mm3, g)
                    after(dve, sum_turned, g - 1)
                    nc.vector.scalar_tensor_tensor(out=sumT[:, :], in0=ps_o[:, :], scalar=const.b3[:, 0:1],
                                                   in1=xT[1 - s][:, :], op0=ALU.add, op1=ALU.add).then_inc(sumT_done, 1)

            def win_next(u, s):
                win.hots(nc, dve, u if s == 0 else u + 1, 1 - s, 2 * u + s + 1)
            steps(dve, step, 3, behind=1)


def edges1(nc, ctx, A, S, const, tab):
    with ExitStack() as own:
        def sb(name, shape, dt=F32):
            return own.enter_context(nc.sbuf_tensor(f"e_{name}", shape, dt))

        def psum(name, parts=P):
            return own.enter_context(nc.psum_tensor(f"e_{name}", [parts, G], F32))

        def sem(name):
            return own.enter_context(nc.semaphore(f"e_{name}"))

        src = [sb(f"src{s}", [P, ROWS], I32) for s in range(2)]
        xs = [sb(f"xs{s}", [P, ROWS * F]) for s in range(2)]
        ea = [sb(f"ea{s}", [P, ROWS * FE]) for s in range(2)]
        xT = sb("xT", [P, G])
        eT = sb("eT", [FE, G])
        z = [sb(f"z{s}", [P, G]) for s in range(2)]
        stats = sb("stats", [P, NG, 6])
        ps_x = [psum(f"ps_x{s}") for s in range(2)]
        ps_e = [psum(f"ps_e{s}", FE) for s in range(2)]
        ps_z = [psum(f"ps_z{s}") for s in range(2)]

        src_in = [sem(f"src_in{s}") for s in range(2)]
        started = sem("started")
        xs_in = [sem(f"xs_in{s}") for s in range(2)]
        ea_in = [sem(f"ea_in{s}") for s in range(2)]
        x_turned, e_turned, xT_done, eT_done, mm, z_done, stats_done = (
            sem(k) for k in ("x_turned", "e_turned", "xT_done", "eT_done", "mm", "z_done", "stats_done"))
        stored = [sem(f"stored{s}") for s in range(2)]
        bn = BatchNormSems(sem)
        bn_bufs = batchnorm_buffers(sb, 1)
        block = own.enter_context(nc.Block())

        @block.sync
        def _(sp):
            def load(u, s, parts=P):
                g = 2 * u + s
                after(sp, x_turned, g - 1)
                rows = A["src"][g * G:g * G + parts * ROWS] if isinstance(g, int) else A["src"][bass.ds(g * G, parts * ROWS)]
                sp.dma_start(src[s][0:parts, :], rows.rearrange("(p k) -> p k", k=ROWS)).then_inc(src_in[s], 16)
                after(sp, e_turned, g - 1)
                sp.dma_start(ea[s][0:parts, :], rows_of(A["edge_attr_64"], g, FE, parts)).then_inc(ea_in[s], 16)
            for u in range(2):
                load(u, 0)
                load(u, 1)
            with sp.Fori(2, PAIRS - 1) as u:
                load(u, 0)
                load(u, 1)
            load(PAIRS - 1, 0)
            load(PAIRS - 1, 1, LAST)

        @block.gpsimd
        def _(pool):
            def step(u, s, valid):
                g = 2 * u + s
                pool.wait_ge(src_in[s], (u + 1) * 16)
                after(pool, x_turned, g - 1)
                pool.sem_inc(started, 1)
                for k in range(ROWS):
                    nc.gpsimd.indirect_dma_start(
                        out=xs[s][:, k * F:(k + 1) * F], out_offset=None, in_=S["x1"][:, :],
                        in_offset=bass.IndirectOffsetOnAxis(ap=src[s][:, k:k + 1], axis=0),
                        bounds_check=N - 1, oob_is_err=True).then_inc(xs_in[s], 16)
            steps(pool, step, 1)

        @block.tensor
        def _(pe):
            def step(u, s, valid):
                g = 2 * u + s
                now, lag1 = valid
                if now:
                    pe.wait_ge(ea_in[s], (u + 1) * 16)
                    after(pe, eT_done, g - 1)
                    pe.wait_ge(xs_in[s], (u + 1) * (16 * ROWS))
                    after(pe, xT_done, g - 1)
                    for k in range(ROWS):
                        op = nc.tensor.transpose(ps_x[s][:, k * P:(k + 1) * P], xs[s][:, k * F:(k + 1) * F], const.ident[:, :])
                    op.then_inc(x_turned, 1)
                    for k in range(ROWS):
                        op = nc.tensor.transpose(ps_e[s][:, k * P:(k + 1) * P], ea[s][:, k * FE:(k + 1) * FE], const.ident[:, :])
                    op.then_inc(e_turned, 1)
                if lag1:
                    pe.wait_ge(eT_done, g)
                    pe.wait_ge(xT_done, g)
                    after(pe, z_done, g - 2)
                    nc.tensor.matmul(ps_z[1 - s][:, :], const.v1x[:, :], xT[:, :], start=True, stop=False)
                    nc.tensor.matmul(ps_z[1 - s][:, :], const.v1e[:, :], eT[:, :], start=False, stop=True).then_inc(mm, 1)
            steps(pe, step, 2)

        @block.scalar
        def _(act):
            def step(u, s, valid):
                g = 2 * u + s
                now, lag1 = valid
                if now:
                    act.wait_ge(x_turned, g + 1)
                    after(act, mm, g)
                    nc.scalar.activation(xT[:, :], ps_x[s][:, :], ACT.Identity).then_inc(xT_done, 1)
                if lag1:
                    act.wait_ge(mm, g)
                    after(act, stats_done, g - 2)
                    if not isinstance(u, int) or g >= 3:
                        act.wait_ge(stored[1 - s], (u - 1 + s) * 16)
                    nc.scalar.activation(z[1 - s][:, :], ps_z[1 - s][:, :], ACT.Identity, bias=const.c1[:, 0:1], scale=1.0).then_inc(z_done, 1)
                    act.wait_ge(z_done, g)
                    act.dma_start(S["z"][bass.ds((g - 1) * P, P), :] if not isinstance(u, int) else S["z"][(g - 1) * P:g * P, :],
                                  z[1 - s][:, :]).then_inc(stored[1 - s], 16)
            steps(act, step, 2)
            for s in range(2):
                act.wait_ge(stored[s], 16 * PAIRS)
            batchnorm_act(nc, act, bn, bn_bufs, const)

        @block.vector
        def _(dve):
            def step(u, s, valid):
                g = 2 * u + s
                now, lag1 = valid
                if now:
                    dve.wait_ge(e_turned, g + 1)
                    after(dve, mm, g)
                    nc.vector.tensor_copy(eT[:, :], ps_e[s][:, :]).then_inc(eT_done, 1)
                if lag1:
                    dve.wait_ge(z_done, g)
                    whole = z[1 - s][:, :]
                    if isinstance(u, int) and g == NG:
                        whole = z[1 - s][:, :].rearrange("f (k p) -> f k p", k=ROWS)[:, :, 0:LAST]
                    to = stats[:, g - 1, :] if isinstance(u, int) else stats[:, bass.ds(g - 1, 1), :].rearrange("p a b -> p (a b)")
                    nc.vector.bn_stats(to, whole).then_inc(stats_done, 1)
            steps(dve, step, 2)
            dve.wait_ge(stats_done, NG)
            batchnorm_dve(nc, dve, bn, bn_bufs, [stats[:, :, :].rearrange("p g s -> p (g s)")],
                          [const.g1[:, 0:1]], [const.be1[:, 0:1]], const.s1, const.t1)


class BatchNormSems:
    def __init__(self, sem):
        self.aggr, self.std, self.scale, self.product, self.shift = (
            sem(k) for k in ("bn_aggr", "bn_std", "bn_scale", "bn_product", "bn_shift"))


def batchnorm_buffers(sb, n):
    return {"mv": sb("bn_mv", [P, n, 2]), "std": sb("bn_std", [P, n]), "inv": sb("bn_inv", [P, n]), "prod": sb("bn_prod", [P, n])}


def batchnorm_dve(nc, dve, bn, b, stats, gammas, betas, scale, shift):
    for m, st in enumerate(stats):
        op = nc.vector.bn_aggr(b["mv"][:, m, :], st)
    op.then_inc(bn.aggr, 1)
    dve.wait_ge(bn.std, 1)
    nc.vector.reciprocal(b["inv"][:, :], b["std"][:, :]).then_inc(bn.scale, 1)
    dve.wait_ge(bn.scale, 1)
    for m in range(len(stats)):
        op = nc.vector.tensor_tensor(scale[:, m:m + 1], b["inv"][:, m:m + 1], gammas[m], ALU.mult)
    op.then_inc(bn.scale, 1)
    dve.wait_ge(bn.scale, 2)
    for m in range(len(stats)):
        op = nc.vector.tensor_tensor(b["prod"][:, m:m + 1], b["mv"][:, m, 0:1], scale[:, m:m + 1], ALU.mult)
    op.then_inc(bn.product, 1)
    dve.wait_ge(bn.product, 1)
    for m in range(len(stats)):
        op = nc.vector.tensor_tensor(shift[:, m:m + 1], betas[m], b["prod"][:, m:m + 1], ALU.subtract)
    op.then_inc(bn.shift, 1)


def batchnorm_act(nc, act, bn, b, const):
    act.wait_ge(bn.aggr, 1)
    nc.scalar.activation(b["std"][:, :], b["mv"][:, :, 1], ACT.Sqrt, bias=const.eps[:, 0:1], scale=1.0).then_inc(bn.std, 1)


def messages1(nc, ctx, A, S, const, tab):
    with ExitStack() as own:
        def sb(name, shape, dt=F32):
            return own.enter_context(nc.sbuf_tensor(f"m_{name}", shape, dt))

        def sem(name):
            return own.enter_context(nc.semaphore(f"m_{name}"))

        z = [sb(f"z{s}", [P, G]) for s in range(2)]
        hT = [sb(f"hT{s}", [P, G]) for s in range(2)]
        h = [sb(f"h{s}", [P, ROWS * F]) for s in range(2)]
        ps = [own.enter_context(nc.psum_tensor(f"m_ps{s}", [P, G], F32)) for s in range(2)]
        z_in = [sem(f"z_in{s}") for s in range(2)]
        stored = [sem(f"stored{s}") for s in range(2)]
        hT_done, turned, h_done = (sem(k) for k in ("hT_done", "turned", "h_done"))
        block = own.enter_context(nc.Block())

        @block.sync
        def _(sp):
            def step(u, s, valid):
                g = 2 * u + s
                after(sp, hT_done, g - 1)
                sp.dma_start(z[s][:, :], S["z"][bass.ds(g * P, P), :] if not isinstance(u, int) else S["z"][g * P:(g + 1) * P, :]).then_inc(z_in[s], 16)
            steps(sp, step, 1)

        @block.scalar
        def _(act):
            def step(u, s, valid):
                g = 2 * u + s
                act.wait_ge(z_in[s], (u + 1) * 16)
                after(act, turned, g - 1)
                nc.scalar.activation(hT[s][:, :], z[s][:, :], ACT.Relu, bias=const.t1[:, 0:1], scale=const.s1[:, 0:1]).then_inc(hT_done, 1)
            steps(act, step, 1)

        @block.tensor
        def _(pe):
            def step(u, s, valid):
                g = 2 * u + s
                pe.wait_ge(hT_done, g + 1)
                after(pe, h_done, g - 1)
                for k in range(ROWS):
                    op = nc.tensor.transpose(ps[s][:, k * P:(k + 1) * P], hT[s][:, k * P:(k + 1) * P], const.ident[:, :])
                op.then_inc(turned, 1)
            steps(pe, step, 1)

        @block.vector
        def _(dve):
            def step(u, s, valid):
                g = 2 * u + s
                dve.wait_ge(turned, g + 1)
                after(dve, stored[s], u * 16)
                nc.vector.tensor_copy(h[s][:, :], ps[s][:, :]).then_inc(h_done, 1)
            steps(dve, step, 1)

        @block.gpsimd
        def _(pool):
            def step(u, s, valid):
                g = 2 * u + s
                pool.wait_ge(h_done, g + 1)
                pool.dma_start(rows_of(S["h"], g, F), h[s][:, :]).then_inc(stored[s], 16)
            steps(pool, step, 1)
            for s in range(2):
                pool.wait_ge(stored[s], 16 * PAIRS)


def nodes1(nc, ctx, A, S, const, tab):
    with ExitStack() as own:
        def sb(name, shape, dt=F32):
            return own.enter_context(nc.sbuf_tensor(f"n_{name}", shape, dt))

        def psum(name):
            return own.enter_context(nc.psum_tensor(f"n_{name}", [P, G], F32))

        def sem(name):
            return own.enter_context(nc.semaphore(f"n_{name}"))

        win = Windows(nc, own, "n", tab, const)
        x = [sb(f"x{s}", [P, ROWS * F]) for s in range(2)]
        xT = sb("xT", [P, G])
        meanT = sb("meanT", [P, G])
        y = [sb(f"y{s}", [P, 2, G]) for s in range(2)]
        stats = sb("stats", [P, 2, NG, 6])
        ps_x, ps_mean, ps_y0, ps_y1 = (psum(k) for k in ("ps_x", "ps_mean", "ps_y0", "ps_y1"))
        ps_y = [ps_y0, ps_y1]
        x_in = [sem(f"x_in{s}") for s in range(2)]
        x_turned, mean_turned, xT_done, meanT_done, stats_done = (
            sem(k) for k in ("x_turned", "mean_turned", "xT_done", "meanT_done", "stats_done"))
        mm = [sem(f"mm{m}") for m in range(2)]
        y_done = [sem(f"y_done{m}") for m in range(2)]
        stored = [sem(f"stored{s}") for s in range(2)]
        bn = BatchNormSems(sem)
        bn_bufs = batchnorm_buffers(sb, 2)
        block = own.enter_context(nc.Block())

        @block.sync
        def _(sp):
            def step(u, s, valid):
                g = 2 * u + s
                now, lag1 = valid
                if now:
                    win.load(nc, sp, u, s, S["h"], S["dscr"])
                    after(sp, x_turned, g - 1)
                    sp.dma_start(x[s][:, :], rows_of(S["x1"], g, F)).then_inc(x_in[s], 16)
                if lag1:
                    win.load_further(nc, sp, g - 1, S["h"], S["dscr"])
            steps(sp, step, 2)

        @block.gpsimd
        def _(pool):
            win.ones(nc, pool)

            def step(u, s, valid):
                win.split(nc, pool, u, s)
                win.split_further(nc, pool, 2 * u + s)
            steps(pool, step, 1)

        @block.tensor
        def _(pe):
            pe.wait_ge(win.ones_done, 4)
            for s in range(2):
                pe.sem_inc(win.xsums_done[s], 1)

            def product(g, m):
                after(pe, y_done[m], g - 1)
                nc.tensor.matmul(ps_y[m][:, :], const.v2[:, 0, m * P:(m + 1) * P], xT[:, :], start=True, stop=False)
                if m == 0:
                    pe.wait_ge(meanT_done, g)
                nc.tensor.matmul(ps_y[m][:, :], const.v2[:, 1, m * P:(m + 1) * P], meanT[:, :], start=False, stop=True).then_inc(mm[m], 1)

            def step(u, s, valid):
                g = 2 * u + s
                now, lag1 = valid
                if lag1:
                    pe.wait_ge(xT_done, g)
                    product(g, 0)
                if now:
                    win.sum_windows(nc, pe, u, s, g, 0)
                if lag1:
                    product(g, 1)
                if now:
                    win.sum_windows(nc, pe, u, s, g, 1)
                    pe.wait_ge(x_in[s], (u + 1) * 16)
                    after(pe, xT_done, g)
                    for k in range(ROWS):
                        op = nc.tensor.transpose(ps_x[:, k * P:(k + 1) * P], x[s][:, k * F:(k + 1) * F], const.ident[:, :])
                    op.then_inc(x_turned, 1)
                    pe.wait_ge(win.mean_done, g + 1)
                    after(pe, meanT_done, g)
                    for j in range(NW):
                        op = nc.tensor.transpose(ps_mean[:, j * P:(j + 1) * P], win.mean[:, j, :], const.ident[:, :])
                    op.then_inc(mean_turned, 1)
            steps(pe, step, 2)

        @block.scalar
        def _(act):
            def step(u, s, valid):
                g = 2 * u + s
                now, lag1 = valid
                if lag1:
                    after(act, stats_done, g - 2)
                    if not isinstance(u, int) or g >= 3:
                        act.wait_ge(stored[1 - s], (u - 1 + s) * 16)
                    for m in range(2):
                        act.wait_ge(mm[m], g)
                        nc.scalar.activation(y[1 - s][:, m, :], ps_y[m][:, :], ACT.Identity, bias=const.c2[:, m:m + 1], scale=1.0).then_inc(y_done[m], 1)
                    for m in range(2):
                        act.wait_ge(y_done[m], g)
                    act.dma_start(S["y"][bass.ds((g - 1) * P, P), :] if not isinstance(u, int) else S["y"][(g - 1) * P:g * P, :],
                                  y[1 - s][:, :, :].rearrange("f m c -> f (m c)")).then_inc(stored[1 - s], 16)
                if now:
                    act.wait_ge(x_turned, g + 1)
                    for m in range(2):
                        after(act, mm[m], g)
                    nc.scalar.activation(xT[:, :], ps_x[:, :], ACT.Identity).then_inc(xT_done, 1)
                    act.wait_ge(mean_turned, g + 1)
                    nc.scalar.activation(meanT[:, :].rearrange("f (k j q) -> f k j q", k=ROWS, j=NW), window_order(ps_mean[:, :]),
                                         ACT.Identity).then_inc(meanT_done, 1)
            steps(act, step, 2)
            for s in range(2):
                act.wait_ge(stored[s], 16 * PAIRS)
            batchnorm_act(nc, act, bn, bn_bufs, const)

        @block.vector
        def _(dve):
            win.hots(nc, dve, 0, 0, 0)

            def step(u, s, valid):
                g = 2 * u + s
                now, lag1 = valid
                if now and not (isinstance(u, int) and g + 1 >= NG):
                    win.hots(nc, dve, u if s == 0 else u + 1, 1 - s, g + 1)
                if lag1:
                    for m in range(2):
                        dve.wait_ge(y_done[m], g)
                        whole = y[1 - s][:, m, :]
                        if isinstance(u, int) and g == NG:
                            whole = whole.rearrange("f (k p) -> f k p", k=ROWS)[:, :, 0:LAST]
                        to = stats[:, m, g - 1, :] if isinstance(u, int) else stats[:, m, bass.ds(g - 1, 1), :].rearrange("p a b -> p (a b)")
                        op = nc.vector.bn_stats(to, whole)
                    op.then_inc(stats_done, 1)
                if now:
                    win.hots_further(nc, dve, g)
                    win.means(nc, dve, g, mean_turned)
            steps(dve, step, 2, behind=1)
            dve.wait_ge(stats_done, NG)
            batchnorm_dve(nc, dve, bn, bn_bufs, [stats[:, m, :, :].rearrange("p g s -> p (g s)") for m in range(2)],
                          [const.g2[:, m:m + 1] for m in range(2)], [const.be2[:, m:m + 1] for m in range(2)], const.s2, const.t2)


def outputs1(nc, ctx, A, S, const, tab, result):
    with ExitStack() as own:
        def sb(name, shape, dt=F32):
            return own.enter_context(nc.sbuf_tensor(f"o_{name}", shape, dt))

        def sem(name):
            return own.enter_context(nc.semaphore(f"o_{name}"))

        y = [sb(f"y{s}", [P, 2 * G]) for s in range(2)]
        x = [sb(f"x{s}", [P, ROWS * F]) for s in range(2)]
        h = [sb(f"h{s}", [P, 2, G]) for s in range(2)]
        o = [sb(f"o{s}", [P, G]) for s in range(2)]
        r = [sb(f"r{s}", [P, ROWS * F]) for s in range(2)]
        stats = sb("stats", [P, ROWS, 6])
        moments = [sb(f"moments{s}", [P, ROWS, 2]) for s in range(2)]
        std = [sb(f"std{s}", [P, ROWS]) for s in range(2)]
        rstd = sb("rstd", [P, ROWS])
        out = [sb(f"out{s}", [P, ROWS * F]) for s in range(2)]
        ps_o = [own.enter_context(nc.psum_tensor(f"o_ps_o{s}", [P, G], F32)) for s in range(2)]
        ps_r = [own.enter_context(nc.psum_tensor(f"o_ps_r{s}", [P, G], F32)) for s in range(2)]
        y_in = [sem(f"y_in{s}") for s in range(2)]
        x_in = [sem(f"x_in{s}") for s in range(2)]
        stored = [sem(f"stored{s}") for s in range(2)]
        h_done, mm, o_done, turned, r_done, stats_done, moments_done, std_done, rstd_done, out_done = (
            sem(k) for k in ("h_done", "mm", "o_done", "turned", "r_done", "stats_done", "moments_done", "std_done", "rstd_done", "out_done"))
        block = own.enter_context(nc.Block())

        @block.sync
        def _(sp):
            def step(u, s, valid):
                g = 2 * u + s
                after(sp, h_done, g - 1)
                sp.dma_start(y[s][:, :], S["y"][bass.ds(g * P, P), :] if not isinstance(u, int) else S["y"][g * P:(g + 1) * P, :]).then_inc(y_in[s], 16)
                after(sp, r_done, g - 1)
                sp.dma_start(x[s][:, :], rows_of(S["x1"], g, F)).then_inc(x_in[s], 16)
            steps(sp, step, 1)

        @block.scalar
        def _(act):
            def step(u, s, valid):
                g = 2 * u + s
                now, lag1, lag2 = valid
                if now:
                    act.wait_ge(y_in[s], (u + 1) * 16)
                    after(act, mm, g - 1)
                    for m in range(2):
                        op = nc.scalar.activation(h[s][:, m, :], y[s][:, m * G:(m + 1) * G], ACT.Relu,
                                                  bias=const.t2[:, m:m + 1], scale=const.s2[:, m:m + 1])
                    op.then_inc(h_done, 1)
                if lag1:
                    act.wait_ge(mm, g)
                    after(act, turned, g - 2)
                    nc.scalar.activation(o[1 - s][:, :], ps_o[1 - s][:, :], ACT.Relu, bias=const.cl[:, 0:1], scale=1.0).then_inc(o_done, 1)
                if lag2:
                    act.wait_ge(moments_done, g - 1)
                    after(act, rstd_done, g - 3)
                    nc.scalar.activation(std[s][:, :], moments[s][:, :, 1], ACT.Sqrt, bias=const.eps[:, 0:1], scale=1.0).then_inc(std_done, 1)
            steps(act, step, 3, ahead=3)

        @block.tensor
        def _(pe):
            def step(u, s, valid):
                g = 2 * u + s
                now, lag1 = valid
                if now:
                    pe.wait_ge(h_done, g + 1)
                    after(pe, o_done, g - 1)
                    nc.tensor.matmul(ps_o[s][:, :], const.vl[:, 0, :], h[s][:, 0, :], start=True, stop=False)
                    nc.tensor.matmul(ps_o[s][:, :], const.vl[:, 1, :], h[s][:, 1, :], start=False, stop=True).then_inc(mm, 1)
                if lag1:
                    pe.wait_ge(o_done, g)
                    after(pe, r_done, g - 2)
                    for k in range(ROWS):
                        op = nc.tensor.transpose(ps_r[1 - s][:, k * P:(k + 1) * P], o[1 - s][:, k * P:(k + 1) * P], const.ident[:, :])
                    op.then_inc(turned, 1)
            steps(pe, step, 2)

        @block.vector
        def _(dve):
            def step(u, s, valid):
                g = 2 * u + s
                _, lag1, lag2, lag3 = valid
                if lag2:
                    dve.wait_ge(turned, g - 1)
                    dve.wait_ge(x_in[s], u * 16)
                    after(dve, out_done, g - 3)
                    nc.vector.tensor_tensor(r[s][:, :], ps_r[s][:, :], x[s][:, :], ALU.add).then_inc(r_done, 1)
                    dve.wait_ge(r_done, g - 1)
                    layernorm_stats(nc, dve, r[s][:, :].rearrange("p (k f) -> p k f", k=ROWS), stats, moments[s],
                                    stats_done, moments_done, g - 2)
                if lag3:
                    dve.wait_ge(std_done, g - 2)
                    after(dve, out_done, g - 3)
                    nc.vector.reciprocal(rstd[:, :], std[1 - s][:, :]).then_inc(rstd_done, 1)
                    dve.wait_ge(rstd_done, g - 2)
                    if not isinstance(u, int) or g >= 5:
                        dve.wait_ge(stored[1 - s], (u - 2 + s) * 16)
                    for k in range(ROWS):
                        op = nc.vector.tensor_scalar(out[1 - s][:, k * F:(k + 1) * F], r[1 - s][:, k * F:(k + 1) * F],
                                                     moments[1 - s][:, k, 0:1], rstd[:, k:k + 1], ALU.subtract, ALU.mult)
                    op.then_inc(out_done, 1)
            steps(dve, step, 4, ahead=3)

        @block.gpsimd
        def _(pool):
            def store(u, s, parts=P):
                g = 2 * u + s
                pool.wait_ge(out_done, g + 1)
                pool.dma_start(rows_of(result, g, F, parts), out[s][0:parts, :]).then_inc(stored[s], 16)
            store(0, 0)
            store(0, 1)
            with pool.Fori(1, PAIRS - 1) as u:
                store(u, 0)
                store(u, 1)
            store(PAIRS - 1, 0)
            store(PAIRS - 1, 1, LAST)
            for s in range(2):
                pool.wait_ge(stored[s], 16 * PAIRS)


def build(nc, A, result):
    with ExitStack() as ctx:
        ctx.enter_context(nc.allow_non_contiguous_dma(reason="single columns of weights and tables"))

        def sb(name, shape, dt=F32):
            return ctx.enter_context(nc.sbuf_tensor(name, shape, dt))

        S = {
            "x1": nc.dram_tensor("s_x1", (NPAD, F), F32).ap(),
            "h": nc.dram_tensor("s_h", (NPAD, F), F32).ap(),
            "z": nc.dram_tensor("s_z", (NG * P, G), F32).ap(),
            "y": nc.dram_tensor("s_y", (NG * P, 2 * G), F32).ap(),
            "dscr": nc.dram_tensor("s_dst", (DSCR, 1), F32).ap(),
            "tabs": nc.dram_tensor("s_tabs", (2, TABW), I32).ap(),
        }
        c = Constants()
        c.ident = sb("ident", [P, P])
        c.node = sb("node", [P, NW, WIN], F16)
        c.minus_first = sb("minus_first", [P, NG])
        c.eps = sb("eps", [P, 1])
        c.w1, c.w2, c.w3 = sb("w1", [P, 2, F]), sb("w2", [P, F]), sb("w3", [P, F])
        c.b1, c.b2, c.b3 = sb("b1", [P, 1]), sb("b2", [P, 1]), sb("b3", [P, 1])
        c.v1x, c.v1e = sb("v1x", [P, F]), sb("v1e", [FE, F])
        c.c1, c.g1, c.be1 = sb("c1", [P, 1]), sb("g1", [P, 1]), sb("be1", [P, 1])
        c.s1, c.t1 = sb("s1", [P, 1]), sb("t1", [P, 1])
        c.v2, c.vl = sb("v2", [P, 2, 2 * F]), sb("vl", [P, 2, F])
        c.c2, c.g2, c.be2, c.cl = sb("c2", [P, 2]), sb("g2", [P, 2]), sb("be2", [P, 2]), sb("cl", [P, 1])
        c.s2, c.t2 = sb("s2", [P, 2]), sb("t2", [P, 2])
        tab = sb("tab", [1, TAB], I32)

        def column(a):
            return a.rearrange("(m p) -> p m", p=P)

        def blocks(a):
            return a.rearrange("(b p) f -> p b f", p=P)

        c.loads = [
            (c.w1[:, :, :], blocks(A["L0_gnn_W1"])), (c.w2[:, :], A["L0_gnn_W2"]), (c.w3[:, :], A["L0_gnn_W3"]),
            (c.b1[:, :], column(A["L0_gnn_b1"])), (c.b2[:, :], column(A["L0_gnn_b2"])), (c.b3[:, :], column(A["L0_gnn_b3"])),
            (c.v1x[:, :], A["L1_gnn_W1"][0:F, :]), (c.v1e[:, :], A["L1_gnn_W1"][F:F + FE, :]),
            (c.c1[:, :], column(A["L1_gnn_b1"])), (c.g1[:, :], column(A["L1_gnn_g1"])), (c.be1[:, :], column(A["L1_gnn_be1"])),
            (c.v2[:, :, :], blocks(A["L1_gnn_W2"])), (c.vl[:, :, :], blocks(A["L1_gnn_Wl"])),
            (c.c2[:, :], column(A["L1_gnn_b2"])), (c.g2[:, :], column(A["L1_gnn_g2"])), (c.be2[:, :], column(A["L1_gnn_be2"])),
            (c.cl[:, :], column(A["L1_gnn_bl"])),
        ]
        with nc.Block() as block:
            @block.vector
            def _(dve):
                nc.vector.memset(c.eps[:, :], EPS)
        prepare(nc, ctx, A, S, c, tab)
        layer0(nc, ctx, A, S, c, tab)
        edges1(nc, ctx, A, S, c, tab)
        messages1(nc, ctx, A, S, c, tab)
        nodes1(nc, ctx, A, S, c, tab)
        outputs1(nc, ctx, A, S, c, tab, result)


_INS = ["x", "src", "dst", "edge_attr_128", "edge_attr_64", "L0_gnn_W1", "L0_gnn_b1", "L0_gnn_W2", "L0_gnn_b2",
        "L0_gnn_W3", "L0_gnn_b3", "L1_gnn_W1", "L1_gnn_b1", "L1_gnn_g1", "L1_gnn_be1", "L1_gnn_W2", "L1_gnn_b2",
        "L1_gnn_g2", "L1_gnn_be2", "L1_gnn_Wl", "L1_gnn_bl"]


def kernel(**inputs):
    import numpy as np
    import concourse.bacc as bacc
    from concourse.bass_utils import run_bass_kernel_spmd

    nc = bacc.Bacc("TRN2", target_bir_lowering=False, num_devices=1)
    arrays, args = {}, {}
    for name in _INS:
        a = np.ascontiguousarray(inputs[name])
        arrays[f"in_{name}"] = a
        args[name] = nc.dram_tensor(f"in_{name}", a.shape, mybir.dt.from_np(a.dtype), kind="ExternalInput").ap()
    result = nc.dram_tensor("out", (N, F), F32, kind="ExternalOutput").ap()
    build(nc, args, result)
    r = run_bass_kernel_spmd(nc, [arrays], core_ids=[0])
    return r.results[0]["out"]
```

```python
from contextlib import ExitStack

import concourse.bass as bass
from concourse import mybir

F32 = mybir.dt.float32
BF16 = mybir.dt.bfloat16
F16 = mybir.dt.float16
I32 = mybir.dt.int32
ALU = mybir.AluOpType
ACT = mybir.ActivationFunctionType
AX_X = mybir.AxisListType.X

P = 128
F = 128
FE = 64
N = 50000
E = 50000
ROWS = 4
G = P * ROWS
NG = -(-N // G)
NPAD = NG * G
LAST = (N - (NG - 1) * G) // ROWS
WIN = 128
NW = G // WIN
TPC = 2
CHUNK = TPC * P
TWO = 36
TABW = 512
TILES = -(-E // P)
BIG = 1.0e9
EXTRA = TILES * P
CLIPS = {n: n * P + (E - CHUNK - n * P) // CHUNK * CHUNK + CHUNK for n in (1, 2)}
DSCR = EXTRA + 6 * CHUNK
TAB_START, TAB_LOOPS, TAB_BEFORE, TAB_ANY = 0, TABW, 2 * TABW, 3 * TABW
TAB = 3 * TABW + P
EPS = 1e-5
PAIRS = NG // 2
UNROLL = 4
QUADS = NG // UNROLL

assert TWO % UNROLL == 0 and NG % 2 == 0 and (N - (NG - 1) * G) % ROWS == 0 and E == N


def after(eng, sem, count, apart=False):
    if not isinstance(count, int) or count > 0:
        if apart and not isinstance(count, int):
            eng.wait_ge(sem, 1)
        eng.wait_ge(sem, count)


def steps(eng, body, stages, ahead=2, behind=0):
    def pair(u):
        for s in range(2):
            i = 2 * u + s if isinstance(u, int) else None
            body(u, s, [True if i is None else 0 <= i - k < NG for k in range(stages)])
    for u in range(ahead):
        pair(u)
    with eng.Fori(ahead, PAIRS - behind) as u:
        pair(u)
    for u in range(PAIRS - behind, PAIRS + stages // 2):
        pair(u)


def quads(eng, body, stages, ahead=1, early=0):
    def turn(u, n=None):
        for s in range(UNROLL):
            i = UNROLL * u + s if isinstance(u, int) else None
            valid = [True if i is None else 0 <= i - k < NG for k in range(-early, stages - early)]
            if any(valid):
                body(u, s, valid, lambda lag, i=i: n if i is None else (TPC if i - lag < TWO else 1))
    edge = TWO // UNROLL
    for u in range(ahead):
        turn(u)
    with eng.Fori(ahead, edge - 1) as u:
        turn(u, TPC)
    turn(edge - 1)
    turn(edge)
    with eng.Fori(edge + 1, QUADS) as u:
        turn(u, 1)
    for u in range(QUADS, -(-(NG + stages) // UNROLL)):
        turn(u)


def place(u, i, ring):
    return i % ring, u * (UNROLL // ring) + (i // ring + 1)


class Windows:

    def __init__(self, nc, ctx, tag, tab, const):
        def sb(name, shape, dt):
            return ctx.enter_context(nc.sbuf_tensor(f"{tag}_{name}", shape, dt))

        def sem(name):
            return ctx.enter_context(nc.semaphore(f"{tag}_{name}"))

        self.tab, self.const = tab, const
        two, four = range(2), range(4)
        self.rows = [sb(f"rows{s}", [P, NW, TPC * F], F32) for s in four]
        self.rest = [sb(f"rest{s}", [P, NW, TPC * F], F32) for s in two]
        self.low = [sb(f"low{s}", [P, NW, TPC, F + 2], BF16) for s in two]
        self.hot = [sb(f"hot{s}", [P, NW, TPC, WIN], BF16) for s in two]
        self.xrows = [sb(f"xrows{s}", [P, TPC * F], F32) for s in two]
        self.xdst = [sb(f"xdst{s}", [P, TPC], F32) for s in two]
        self.xrest = [sb(f"xrest{s}", [P, TPC * F], F32) for s in two]
        self.xlow = [sb(f"xlow{s}", [P, TPC, F + 2], BF16) for s in two]
        self.xhot = [sb(f"xhot{s}", [P, TPC, WIN], BF16) for s in two]
        self.count = sb("count", [P, NW], F32)
        self.inv = sb("inv", [P, NW], F32)
        self.mean = sb("mean", [P, NW, F], F32)
        self.sums = [ctx.enter_context(nc.psum_tensor(f"{tag}_sums{b}", [P, 2, F + 1], F32)) for b in two]
        self.rows_in = [sem(f"rows_in{s}") for s in four]
        self.dst = None
        self.dst_in = [sem(f"dst_in{s}") for s in four]
        self.near_done = sem("near_done")
        self.xrows_in = [sem(f"xrows_in{s}") for s in two]
        self.rest_done = sem("rest_done")
        self.split_done = sem("split_done")
        self.xrest_done = sem("xrest_done")
        self.xsplit_done = [sem(f"xsplit_done{s}") for s in two]
        self.hot_done = sem("hot_done")
        self.xhot_done = [sem(f"xhot_done{s}") for s in two]
        self.sums_done = sem("sums_done")
        self.xsums_done = [sem(f"xsums_done{s}") for s in two]
        self.count_done = sem("count_done")
        self.inv_done = sem("inv_done")
        self.mean_done = sem("mean_done")
        self.ones_done = sem("ones_done")

    def further(self, nc, eng, g, body):
        tab = self.tab
        some = eng.value_load(tab[0:1, bass.ds(g + TAB_ANY, 1)], min_val=0, max_val=1 << 20)
        with eng.If(some > 0):
            for j in range(NW):
                w = g * NW + j
                loops = eng.value_load(tab[0:1, bass.ds(w + TAB_LOOPS, 1)], min_val=0, max_val=1 << 20)
                before = eng.value_load(tab[0:1, bass.ds(w + TAB_BEFORE, 1)], min_val=0, max_val=1 << 20)
                with eng.If(loops > 0):
                    with eng.Fori(0, loops) as t:
                        body(j, t, before + t)
                    eng.nop()
                eng.nop()
            eng.nop()

    def load(self, nc, sp, u, s, tiles, src, dscr):
        g = UNROLL * u + s
        slot, _ = place(u, s, 4)
        after(sp, self.sums_done, g - 3, apart=True)
        for j in range(NW):
            start = sp.value_load(self.tab[0:1, bass.ds(g * NW + (TAB_START + j), 1)], min_val=0, max_val=E - tiles * P)
            sp.dma_start(self.rows[slot][:, j, 0:tiles * F],
                         src[bass.ds(start, tiles * P), :].rearrange("(p t) f -> p (t f)", t=tiles)).then_inc(self.rows_in[slot], 16)
            if self.dst:
                if j == 0:
                    after(sp, self.near_done, g - 3, apart=True)
                sp.dma_start(self.dst[slot][:, j, 0:tiles],
                             dscr[bass.ds(start, tiles * P), :].rearrange("(p t) o -> p (t o)", t=tiles)).then_inc(self.dst_in[slot], 16)

    def load_further(self, nc, sp, g, tiles, src, dscr):
        def body(j, t, turn):
            start = sp.value_load(self.tab[0:1, bass.ds(g * NW + (TAB_START + j), 1)], min_val=0, max_val=E - tiles * P)
            for s in range(2):
                after(sp, self.xsums_done[s], turn + 1, apart=True)
                pos = sp.snap(start + t * (2 * CHUNK) + (tiles * P + s * CHUNK))
                with sp.If(pos > E - CHUNK):
                    sp.dma_start(self.xrows[s][:, :],
                                 src[E - CHUNK:E, :].rearrange("(p t) f -> p (t f)", t=TPC)).then_inc(self.xrows_in[s], 16)
                    shift = EXTRA + (tiles - 1) * 3 * CHUNK - CLIPS[tiles]
                    far = (pos + shift).with_bounds(min_val=0, max_val=DSCR - CHUNK)
                    sp.dma_start(self.xdst[s][:, :],
                                 dscr[bass.ds(far, CHUNK), :].rearrange("(p t) o -> p (t o)", t=TPC)).then_inc(self.xrows_in[s], 16)
                with sp.Else():
                    near = (pos + 0).with_bounds(min_val=0, max_val=E - CHUNK)
                    sp.dma_start(self.xrows[s][:, :],
                                 src[bass.ds(near, CHUNK), :].rearrange("(p t) f -> p (t f)", t=TPC)).then_inc(self.xrows_in[s], 16)
                    sp.dma_start(self.xdst[s][:, :],
                                 dscr[bass.ds(near, CHUNK), :].rearrange("(p t) o -> p (t o)", t=TPC)).then_inc(self.xrows_in[s], 16)
                sp.nop()
        self.further(nc, sp, g, body)

    def ones(self, nc, pool):
        for s in range(2):
            nc.gpsimd.memset(self.low[s][:, :, :, F:F + 2], 1.0).then_inc(self.ones_done, 1)
            nc.gpsimd.memset(self.xlow[s][:, :, F:F + 2], 1.0).then_inc(self.ones_done, 1)

    def split(self, nc, pool, u, s, tiles):
        g = UNROLL * u + s
        slot, use = place(u, s, 4)
        pair, _ = place(u, s, 2)
        pool.wait_ge(self.rows_in[slot], use * (16 * NW))
        after(pool, self.sums_done, g - 1)
        rows, rest = self.rows[slot][:, :, 0:tiles * F], self.rest[pair][:, :, 0:tiles * F]
        nc.gpsimd.tensor_tensor(rest, rows, upper(rows), ALU.subtract).then_inc(self.rest_done, 1)
        pool.wait_ge(self.rest_done, g + 1)
        nc.gpsimd.tensor_tensor(self.low[pair][:, :, 0:tiles, 0:F], rest.rearrange("p j (t f) -> p j t f", t=tiles),
                                upper(rest).rearrange("p j (t f) -> p j t f", t=tiles),
                                ALU.subtract).then_inc(self.split_done, 1)

    def split_further(self, nc, pool, g):
        def body(j, t, turn):
            for s in range(2):
                pool.wait_ge(self.xrows_in[s], (turn + 1) * 32)
                rows, rest = self.xrows[s][:, :], self.xrest[s][:, :]
                nc.gpsimd.tensor_tensor(rest, rows, upper(rows), ALU.subtract).then_inc(self.xrest_done, 1)
                pool.wait_ge(self.xrest_done, turn * 2 + (s + 1))
                nc.gpsimd.tensor_tensor(self.xlow[s][:, :, 0:F], rest.rearrange("p (t f) -> p t f", t=TPC),
                                        upper(rest).rearrange("p (t f) -> p t f", t=TPC),
                                        ALU.subtract).then_inc(self.xsplit_done[s], 1)
        self.further(nc, pool, g, body)

    def to_near(self, nc, dve, u, s, tiles):
        g = UNROLL * u + s
        slot, use = place(u, s, 4)
        dve.wait_ge(self.dst_in[slot], use * (16 * NW))
        c = self.const
        nc.vector.tensor_tensor(c.near[:, bass.ds(g * NW, NW), 0:tiles], self.dst[slot][:, :, 0:tiles],
                                c.window_first[:, bass.ds(g * NW, NW)].unsqueeze(2).to_broadcast([P, NW, tiles]),
                                ALU.subtract).then_inc(self.near_done, 1)
        dve.wait_ge(self.near_done, g + 1)

    def hots(self, nc, dve, u, s, tiles):
        g = UNROLL * u + s
        pair, _ = place(u, s, 2)
        after(dve, self.sums_done, g - 1)
        if self.dst:
            self.to_near(nc, dve, u, s, tiles)
        for j in range(NW):
            for t in range(tiles):
                op = nc.vector.tensor_scalar(self.hot[pair][:, j, t, :], self.const.node_w[:, :],
                                             self.const.near[:, bass.ds(g * NW + j, 1), t:t + 1].rearrange("p a b -> p (a b)"),
                                             None, ALU.is_equal)
        op.then_inc(self.hot_done, 1)

    def hots_further(self, nc, dve, g):
        def body(j, t, turn):
            for s in range(2):
                dve.wait_ge(self.xrows_in[s], (turn + 1) * 32)
                for k in range(TPC):
                    op = nc.vector.tensor_scalar(self.xhot[s][:, k, :], self.const.node[:, j, :], self.xdst[s][:, k:k + 1],
                                                 self.const.minus_first[:, bass.ds(g, 1)], ALU.subtract, ALU.is_equal)
                op.then_inc(self.xhot_done[s], 1)
        self.further(nc, dve, g, body)

    def sum_tile(self, nc, out, hot, rows, rest, low, start, stop, further=False):
        nc.tensor.matmul(out, hot, low, start=start, stop=False, skip_group_check=further)
        nc.tensor.matmul(out[:, 0:F], hot, rows, start=False, stop=False, skip_group_check=further)
        return nc.tensor.matmul(out[:, 0:F], hot, rest, start=False, stop=stop, skip_group_check=further)

    def sum_windows(self, nc, pe, u, s, tiles, half):
        g = UNROLL * u + s
        slot, _ = place(u, s, 4)
        pair, _ = place(u, s, 2)
        if half == 0:
            pe.wait_ge(self.hot_done, g + 1)
            pe.wait_ge(self.split_done, g + 1)
            after(pe, self.mean_done, g)
        for j in (2 * half, 2 * half + 1):
            for t in range(tiles):
                last = half == 1 and j == NW - 1 and t == tiles - 1
                if last:
                    self.sum_further(nc, pe, g)
                mm = self.sum_tile(nc, self.sums[half][:, j % 2, :], self.hot[pair][:, j, t, :],
                                   upper(self.rows[slot][:, j, t * F:(t + 1) * F]), upper(self.rest[pair][:, j, t * F:(t + 1) * F]),
                                   self.low[pair][:, j, t, 0:F + 1], start=(j % 2 == 0 and t == 0),
                                   stop=(j % 2 == 1 and t == tiles - 1))
        if half == 1:
            mm.then_inc(self.sums_done, 1)

    def sum_further(self, nc, pe, g):
        def body(j, t, turn):
            for s in range(2):
                pe.wait_ge(self.xhot_done[s], turn + 1)
                pe.wait_ge(self.xsplit_done[s], turn + 1)
                for k in range(TPC):
                    mm = self.sum_tile(nc, self.sums[j // 2][:, j % 2, :], self.xhot[s][:, k, :],
                                       upper(self.xrows[s][:, k * F:(k + 1) * F]), upper(self.xrest[s][:, k * F:(k + 1) * F]),
                                       self.xlow[s][:, k, 0:F + 1], start=False, stop=False, further=True)
                mm.then_inc(self.xsums_done[s], 1)
        self.further(nc, pe, g, body)

    def means(self, nc, dve, g, mean_read):
        dve.wait_ge(self.sums_done, g + 1)
        for b in range(2):
            op = nc.vector.tensor_scalar(self.count[:, 2 * b:2 * b + 2], self.sums[b][:, :, F], 1.0, None, ALU.max)
        op.then_inc(self.count_done, 1)
        dve.wait_ge(self.count_done, g + 1)
        nc.vector.reciprocal(self.inv[:, :], self.count[:, :]).then_inc(self.inv_done, 1)
        dve.wait_ge(self.inv_done, g + 1)
        after(dve, mean_read, g)
        for b in range(2):
            op = nc.vector.tensor_tensor(self.mean[:, 2 * b:2 * b + 2, :], self.sums[b][:, :, 0:F],
                                         self.inv[:, 2 * b:2 * b + 2].unsqueeze(2).to_broadcast([P, 2, F]), ALU.mult)
        op.then_inc(self.mean_done, 1)


def upper(ap):
    v = ap.bitcast(BF16)
    if len(v.shape) == 2:
        return v[:, 1::2]
    return v[:, :, 1::2]


class Constants:
    pass


def rows_of(dram, g, width, parts=P):
    if isinstance(g, int):
        view = dram[g * G:g * G + parts * ROWS, :]
    else:
        view = dram[bass.ds(g * G, parts * ROWS), :]
    return view.rearrange("(p k) f -> p (k f)", k=ROWS)


def panel(dram, g):
    return dram[g * P:(g + 1) * P, :] if isinstance(g, int) else dram[bass.ds(g * P, P), :]


def window_order(ap):
    return ap.rearrange("f (j k q) -> f k j q", j=NW, k=ROWS)


def prepare(nc, ctx, A, S, const, tab):
    with ExitStack() as own:
        def sb(name, shape, dt):
            return own.enter_context(nc.sbuf_tensor(f"t_{name}", shape, dt))

        def sem(name):
            return own.enter_context(nc.semaphore(f"t_{name}"))

        DP = 125
        DR = E // DP
        C8 = 2 * TABW // P
        CW = TABW // P
        d0 = sb("d0", [DP, DR], I32)
        d1 = sb("d1", [DP, DR], I32)
        f0 = sb("f0", [DP, DR], F32)
        f1 = sb("f1", [DP, DR], F32)
        down = sb("down", [DP, DR], F32)
        falls = sb("falls", [P, 1], F32)
        unsorted = sb("unsorted", [P, 1], F32)
        sorted_ = sb("sorted", [P, 1], F32)
        heads_i = sb("heads_i", [1, TILES], I32)
        heads = sb("heads", [1, TILES], F32)
        heads_all = sb("heads_all", [P, TILES], F32)
        below = sb("below", [P, TILES], F32)
        ones = sb("ones", [P, P], F32)
        thr_i = sb("thr_i", [P, C8], I32)
        thr = sb("thr", [P, C8], F32)
        whole = sb("whole", [P, C8], F32)
        row = sb("row", [P, C8], F32)
        row_i = sb("row_i", [P, C8], I32)
        tile = sb("tile", [P, C8, P], F32)
        under = sb("under", [P, C8, P], F32)
        part = sb("part", [P, C8], F32)
        pos = sb("pos", [P, C8], F32)
        size = sb("size", [P, CW], F32)
        size_i = sb("size_i", [P, CW], I32)
        loops_i = sb("loops_i", [P, CW], I32)
        loops = sb("loops", [P, CW], F32)
        start = sb("start", [P, CW], F32)
        start_i = sb("start_i", [P, CW], I32)
        far = sb("far", [1, DSCR - E], F32)
        tail_i = sb("tail_i", [1, CHUNK], I32)
        caps = sb("caps", [P, CW], F32)
        bias = [sb(f"bias{k}", [3, 2, F], F32) for k in range(6)]
        line = sb("line", [1, 2, TABW], I32)
        run = [sb(f"run{k}", [1, TABW], F32) for k in range(2)]
        lone = sb("lone", [1, TABW], F32)
        node_i = sb("node_i", [P, NW, WIN], I32)
        first_i = sb("first_i", [P, NG], I32)
        window_i = sb("window_i", [P, NG * NW], I32)
        ps_falls = own.enter_context(nc.psum_tensor("t_ps_falls", [P, 1], F32))
        ps_heads = own.enter_context(nc.psum_tensor("t_ps_heads", [P, TILES], F32))

        loaded = sem("loaded")
        weights_in = sem("weights_in")
        filled = sem("filled")
        made = sem("made")
        heads_done = sem("heads_done")
        spread = sem("spread")
        written = sem("written")
        rows_done = sem("rows_done")
        gathered = sem("gathered")
        found = sem("found")
        tables_out = sem("tables_out")
        tables_in = sem("tables_in")
        v = sem("v")
        block = own.enter_context(nc.Block())

        @block.sync
        def _(sp):
            dst = A["dst"]
            sp.dma_start(d0[:, :], dst.rearrange("(p r) -> p r", p=DP)).then_inc(loaded, 16)
            sp.dma_start(heads_i[:, 0:TILES - 1],
                         dst[0:(TILES - 1) * P].rearrange("(o i s) -> o i s", o=1, s=P)[:, :, 0]).then_inc(loaded, 16)
            sp.dma_start(heads_i[:, TILES - 1:TILES],
                         dst[(TILES - 1) * P:(TILES - 1) * P + 1].rearrange("(o i) -> o i", o=1)).then_inc(loaded, 16)
            sp.dma_start(tail_i[:, :], dst[E - CHUNK:E].rearrange("(o i) -> o i", o=1)).then_inc(loaded, 16)
            sp.dma_start(d1[0:DP - 1, :], dst[1:1 + (DP - 1) * DR].rearrange("(p r) -> p r", r=DR)).then_inc(loaded, 16)
            sp.dma_start(d1[DP - 1:DP, 0:DR - 1], dst[1 + (DP - 1) * DR:E].rearrange("(o r) -> o r", o=1)).then_inc(loaded, 16)
            sp.dma_start(d1[DP - 1:DP, DR - 1:DR], dst[E - 1:E].rearrange("(o r) -> o r", o=1)).then_inc(loaded, 16)
            for to, what in const.loads:
                sp.dma_start(to, what).then_inc(weights_in, 16)
            sp.wait_ge(made, 1)
            sp.dma_start(S["dscr"][0:E, :].rearrange("(p r) o -> p (r o)", p=DP), f0[:, :]).then_inc(written, 16)
            sp.dma_start(S["dscr"][E:DSCR, :].rearrange("(q r) o -> q (r o)", q=1), far[:, :]).then_inc(written, 16)
            sp.wait_ge(found, 1)
            sp.dma_start(S["tabs"][0:1, :].rearrange("o (c p) -> p (o c)", p=P), start_i[:, :]).then_inc(tables_out, 16)
            sp.dma_start(S["tabs"][1:2, :].rearrange("o (c p) -> p (o c)", p=P), loops_i[:, :]).then_inc(tables_out, 16)
            sp.wait_ge(tables_out, 32)
            sp.dma_start(line[:, :, :], S["tabs"].rearrange("(o t) w -> o t w", o=1)).then_inc(tables_in, 16)

        @block.gpsimd
        def _(pool):
            nc.gpsimd.iota(node_i[:, :, :].rearrange("p j (k q) -> p j k q", k=ROWS),
                           [[WIN, NW], [1, ROWS], [ROWS, WIN // ROWS]], base=0, channel_multiplier=0).then_inc(filled, 1)
            nc.gpsimd.iota(first_i[:, :], [[-G, NG]], base=0, channel_multiplier=0).then_inc(filled, 1)
            nc.gpsimd.iota(thr_i[:, 0:CW], [[P * WIN, CW]], base=0, channel_multiplier=WIN).then_inc(filled, 1)
            nc.gpsimd.iota(thr_i[:, CW:C8], [[P * WIN, CW]], base=WIN, channel_multiplier=WIN).then_inc(filled, 1)
            nc.gpsimd.iota(window_i[:, :], [[WIN, NG * NW]], base=0, channel_multiplier=0).then_inc(filled, 1)
            nc.gpsimd.memset(ones[:, :], 1.0).then_inc(filled, 1)
            nc.gpsimd.memset(const.ident[:, :], 0.0).then_inc(filled, 1)
            pool.wait_ge(filled, 7)
            nc.gpsimd.affine_select(out=const.ident[:, :], in_=const.ident[:, :], compare_op=ALU.not_equal, fill=1.0,
                                    base=0, pattern=[[-1, P]], channel_multiplier=1).then_inc(filled, 1)
            pool.wait_ge(written, 32)
            pool.wait_ge(rows_done, 1)
            for c in range(C8):
                nc.gpsimd.indirect_dma_start(
                    out=tile[:, c, :], out_offset=None,
                    in_=S["dscr"][0:TILES * P, :].rearrange("(i s) o -> i (s o)", s=P),
                    in_offset=bass.IndirectOffsetOnAxis(ap=row_i[:, c:c + 1], axis=0),
                    bounds_check=TILES - 1, oob_is_err=True).then_inc(gathered, 16)
            pool.wait_ge(gathered, 16 * C8)

        @block.tensor
        def _(pe):
            pe.wait_ge(filled, 7)
            pe.wait_ge(heads_done, 1)
            nc.tensor.matmul(ps_heads[:, :], ones[0:1, :], heads[:, :], start=True, stop=True).then_inc(spread, 1)
            pe.wait_ge(heads_done, 2)
            nc.tensor.matmul(ps_falls[:, :], ones[0:DP, :], falls[0:DP, :], start=True, stop=True).then_inc(spread, 1)

        @block.vector
        def _(dve):
            n = [0]

            def then(op):
                n[0] += 1
                op.then_inc(v, 1)
                dve.wait_ge(v, n[0])

            dve.wait_ge(loaded, 16 * 7)
            nc.vector.tensor_copy(heads[:, :], heads_i[:, :]).then_inc(heads_done, 1)
            then(nc.vector.memset(far[:, :], BIG))
            for tiles in (1, 2):
                end = EXTRA - E + (tiles - 1) * 3 * CHUNK + CHUNK
                then(nc.vector.tensor_copy(far[:, end - (E - CLIPS[tiles]):end], tail_i[:, CHUNK - (E - CLIPS[tiles]):CHUNK]))
            nc.vector.tensor_copy(f1[:, :], d1[:, :])
            then(nc.vector.tensor_copy(f0[:, :], d0[:, :]))
            nc.vector.tensor_tensor(down[:, :], f0[:, :], f1[:, :], ALU.is_gt).then_inc(made, 1)
            dve.wait_ge(made, 1)
            nc.vector.tensor_reduce(falls[0:DP, :], down[:, :], AX_X, ALU.add).then_inc(heads_done, 1)
            dve.wait_ge(filled, 8)
            nc.vector.tensor_copy(const.node[:, :, :], node_i[:, :, :])
            nc.vector.tensor_copy(const.node_w[:, :], node_i[:, 0, :])
            nc.vector.tensor_copy(const.minus_first[:, :], first_i[:, :])
            nc.vector.tensor_copy(const.window_first[:, :], window_i[:, :])
            nc.vector.tensor_copy(thr[:, :], thr_i[:, :])
            dve.wait_ge(spread, 2)
            nc.vector.tensor_scalar(unsorted[:, :], ps_falls[:, :], 0.5, None, ALU.is_gt)
            nc.vector.tensor_scalar(sorted_[:, :], ps_falls[:, :], 0.5, None, ALU.is_lt)
            then(nc.vector.tensor_copy(heads_all[:, :], ps_heads[:, :]))
            for c in range(C8):
                then(nc.vector.tensor_scalar(below[:, :], heads_all[:, :], thr[:, c:c + 1], None, ALU.is_lt))
                then(nc.vector.tensor_reduce(whole[:, c:c + 1], below[:, :], AX_X, ALU.add))
            then(nc.vector.tensor_scalar(row[:, :], whole[:, :], -1.0, 0.0, ALU.add, ALU.max))
            nc.vector.tensor_copy(row_i[:, :], row[:, :]).then_inc(rows_done, 1)
            dve.wait_ge(gathered, 16 * C8)
            for c in range(C8):
                then(nc.vector.tensor_scalar(under[:, c, :], tile[:, c, :], thr[:, c:c + 1], None, ALU.is_lt))
            then(nc.vector.tensor_reduce(part[:, :], under[:, :, :], AX_X, ALU.add))
            then(nc.vector.scalar_tensor_tensor(out=pos[:, :], in0=row[:, :], scalar=float(P), in1=part[:, :],
                                                op0=ALU.mult, op1=ALU.add))
            then(nc.vector.tensor_scalar(pos[:, :], pos[:, :], sorted_[:, 0:1], None, ALU.mult))
            then(nc.vector.tensor_scalar(whole[:, 0:1], unsorted[:, :], float(E), None, ALU.mult))
            then(nc.vector.tensor_scalar(pos[:, CW:C8], pos[:, CW:C8], whole[:, 0:1], None, ALU.add))
            then(nc.vector.tensor_scalar(caps[:, :], thr[:, 0:CW], float(TWO * G), float(CHUNK - P), ALU.is_ge, ALU.mult))
            then(nc.vector.tensor_scalar(caps[:, :], caps[:, :], float(-CHUNK), None, ALU.add))
            then(nc.vector.tensor_tensor(size[:, :], pos[:, CW:C8], pos[:, 0:CW], ALU.subtract))
            then(nc.vector.tensor_tensor(size[:, :], size[:, :], caps[:, :], ALU.add))
            then(nc.vector.tensor_scalar(size[:, :], size[:, :], 0.0, None, ALU.max))
            then(nc.vector.tensor_scalar(size[:, :], size[:, :], float(2 * CHUNK - 1), None, ALU.add))
            then(nc.vector.tensor_copy(size_i[:, :], size[:, :]))
            then(nc.vector.tensor_scalar(loops_i[:, :], size_i[:, :], (2 * CHUNK).bit_length() - 1, None, ALU.logical_shift_right))
            then(nc.vector.tensor_copy(loops[:, :], loops_i[:, :]))
            then(nc.vector.tensor_scalar(loops[:, :], loops[:, :], float(-2 * CHUNK), float(E), ALU.mult, ALU.add))
            then(nc.vector.tensor_tensor(loops[:, :], loops[:, :], caps[:, :], ALU.add))
            then(nc.vector.tensor_tensor(start[:, :], pos[:, 0:CW], loops[:, :], ALU.min))
            then(nc.vector.tensor_scalar(start[:, :], start[:, :], 0.0, None, ALU.max))
            nc.vector.tensor_copy(start_i[:, :], start[:, :]).then_inc(found, 1)
            dve.wait_ge(tables_in, 16)
            then(nc.vector.tensor_copy(tab[:, TAB_START:TAB_START + TABW], line[:, 0, :]))
            then(nc.vector.tensor_copy(tab[:, TAB_LOOPS:TAB_LOOPS + TABW], line[:, 1, :]))
            then(nc.vector.tensor_copy(lone[:, :], line[:, 1, :]))
            then(nc.vector.tensor_copy(run[0][:, :], line[:, 1, :]))
            reach, k = 1, 0
            while reach < TABW:
                then(nc.vector.tensor_copy(run[1 - k][:, 0:reach], run[k][:, 0:reach]))
                then(nc.vector.tensor_tensor(run[1 - k][:, reach:TABW], run[k][:, reach:TABW],
                                             run[k][:, 0:TABW - reach], ALU.add))
                reach, k = 2 * reach, 1 - k
            then(nc.vector.tensor_tensor(run[1 - k][:, :], run[k][:, :], lone[:, :], ALU.subtract))
            then(nc.vector.tensor_copy(tab[:, TAB_BEFORE:TAB_BEFORE + TABW], run[1 - k][:, :]))
            then(nc.vector.tensor_reduce(run[k][:, 0:P], lone[:, :].rearrange("o (g j) -> o g j", j=NW), AX_X, ALU.add))
            then(nc.vector.tensor_copy(tab[:, TAB_ANY:TAB_ANY + P], run[k][:, 0:P]))
            dve.wait_ge(weights_in, 16 * len(const.loads))
            x, r1, r2, a0, a1, a2 = (b[:, :, :] for b in bias)
            then(nc.vector.tensor_copy(x, const.brow[:, :, :]))
            then(nc.vector.tensor_tensor(r1, x, upper(x), ALU.subtract))
            then(nc.vector.tensor_tensor(r2, r1, upper(r1), ALU.subtract))
            then(nc.vector.tensor_scalar(a0, upper(x), const.ident[0:3, 0:1], None, ALU.mult))
            then(nc.vector.scalar_tensor_tensor(out=a1, in0=upper(r1), scalar=const.ident[0:3, 1:2], in1=a0, op0=ALU.mult, op1=ALU.add))
            then(nc.vector.scalar_tensor_tensor(out=a2, in0=r2, scalar=const.ident[0:3, 2:3], in1=a1, op0=ALU.mult, op1=ALU.add))
            for k in range(ROWS):
                nc.vector.tensor_copy(const.bias3[:, :, k * F:(k + 1) * F], a2)
            nc.vector.memset(const.ones3[:, :], 1.0)


class Norm:

    def __init__(self, sb, sem):
        self.stats = sb("stats", [P, ROWS, 6])
        self.moments = sb("moments", [P, ROWS, 2])
        self.std, self.rstd, self.shift = (sb(k, [P, ROWS]) for k in ("std", "rstd", "shift"))
        self.stats_done, self.moments_done, self.std_done, self.rstd_done, self.shift_done = (
            sem(k) for k in ("stats_done", "moments_done", "std_done", "rstd_done", "shift_done"))

    def moments_of(self, nc, dve, rows, g):
        for k in range(ROWS):
            op = nc.vector.bn_stats(self.stats[:, k, :], rows[:, k * F:(k + 1) * F])
        op.then_inc(self.stats_done, 1)
        after(dve, self.stats_done, g + 1, apart=True)
        for k in range(ROWS):
            op = nc.vector.bn_aggr(self.moments[:, k, :], self.stats[:, k, :])
        op.then_inc(self.moments_done, 1)

    def deviations(self, nc, act, const, g):
        act.wait_ge(self.moments_done, g + 1)
        nc.scalar.activation(self.std[:, :], self.moments[:, :, 1], ACT.Sqrt, bias=const.eps[:, 0:1], scale=1.0).then_inc(self.std_done, 1)

    def scales(self, nc, dve, g, out_done):
        dve.wait_ge(self.std_done, g + 1)
        after(dve, out_done, g)
        nc.vector.reciprocal(self.rstd[:, :], self.std[:, :]).then_inc(self.rstd_done, 1)
        dve.wait_ge(self.rstd_done, g + 1)
        nc.vector.scalar_tensor_tensor(out=self.shift[:, :], in0=self.moments[:, :, 0], scalar=-1.0, in1=self.rstd[:, :],
                                       op0=ALU.mult, op1=ALU.mult).then_inc(self.shift_done, 1)

    def normalise(self, nc, act, g, out, rows, stored, use, out_done):
        act.wait_ge(self.shift_done, g + 1)
        after(act, stored, (use - 1) * 16)
        for k in range(ROWS):
            op = nc.scalar.activation(out[:, k * F:(k + 1) * F], rows[:, k * F:(k + 1) * F], ACT.Identity,
                                      bias=self.shift[:, k:k + 1], scale=self.rstd[:, k:k + 1])
        op.then_inc(out_done, 1)


def layer0(nc, ctx, A, S, const, tab):
    with ExitStack() as own:
        def sb(name, shape, dt=F32):
            return own.enter_context(nc.sbuf_tensor(f"a_{name}", shape, dt))

        def psum(name):
            return own.enter_context(nc.psum_tensor(f"a_{name}", [P, G], F32))

        def sem(name):
            return own.enter_context(nc.semaphore(f"a_{name}"))

        win = Windows(nc, own, "a", tab, const)
        win.dst = [sb(f"dst{s}", [P, NW, TPC]) for s in range(4)]
        x = [sb(f"x{s}", [P, ROWS * F]) for s in range(4)]
        xT = [sb(f"xT{s}", [P, G]) for s in range(2)]
        meanT = sb("meanT", [P, G])
        h1 = sb("h1", [P, G])
        h2 = [sb(f"h2{s}", [P, G]) for s in range(2)]
        r = [sb(f"r{s}", [P, ROWS * F]) for s in range(2)]
        norm = Norm(sb, sem)
        out = [sb(f"out{s}", [P, ROWS * F]) for s in range(2)]
        ps_x, ps_mean, ps_h1, ps_h2, ps_o = (psum(k) for k in ("ps_x", "ps_mean", "ps_h1", "ps_h2", "ps_o"))

        x_in = [sem(f"x_in{s}") for s in range(4)]
        x_turned, mean_turned, xT_done, meanT_done = (sem(k) for k in ("x_turned", "mean_turned", "xT_done", "meanT_done"))
        mm1, h1_done, mm2, h2_done, mm3 = (sem(k) for k in ("mm1", "h1_done", "mm2", "h2_done", "mm3"))
        r_done, out_done = (sem(k) for k in ("r_done", "out_done"))
        stored = [sem(f"stored{s}") for s in range(2)]
        block = own.enter_context(nc.Block())

        @block.sync
        def _(sp):
            def step(u, s, valid, tiles):
                g = UNROLL * u + s
                now, lag1, lag2 = valid
                if now:
                    win.load(nc, sp, u, s, tiles(0), A["edge_attr_128"], S["dscr"])
                if lag2:
                    win.load_further(nc, sp, g - 2, tiles(2), A["edge_attr_128"], S["dscr"])
                if lag1:
                    slot, _ = place(u, s - 1, 4)
                    parts = LAST if isinstance(g, int) and g == NG else P
                    after(sp, r_done, g - 4)
                    sp.dma_start(x[slot][0:parts, :], rows_of(A["x"], g - 1, F, parts)).then_inc(x_in[slot], 16)
            quads(sp, step, 3, ahead=2)

        @block.gpsimd
        def _(pool):
            win.ones(nc, pool)

            def step(u, s, valid, tiles):
                win.split(nc, pool, u, s, tiles(0))
                win.split_further(nc, pool, UNROLL * u + s)
            quads(pool, step, 1)

        @block.tensor
        def _(pe):
            pe.wait_ge(win.ones_done, 4)
            for s in range(2):
                pe.sem_inc(win.xsums_done[s], 1)

            def step(u, s, valid, tiles):
                g = UNROLL * u + s
                now, lag1, lag2 = valid
                if lag1:
                    slot, _ = place(u, s - 1, 2)
                    pe.wait_ge(win.mean_done, g)
                    after(pe, meanT_done, g - 1)
                    for j in range(NW):
                        mm = nc.tensor.transpose(ps_mean[:, j * P:(j + 1) * P], win.mean[:, j, :], const.ident[:, :])
                    mm.then_inc(mean_turned, 1)
                    pe.wait_ge(xT_done, g)
                    after(pe, h1_done, g - 1)
                    nc.tensor.matmul(ps_h1[:, :], const.w1[:, 0, :], xT[slot][:, :], start=True, stop=False)
                    pe.wait_ge(meanT_done, g)
                    nc.tensor.matmul(ps_h1[:, :], const.w1[:, 1, :], meanT[:, :], start=False, stop=True).then_inc(mm1, 1)
                if now:
                    slot, use = place(u, s, 4)
                    pe.wait_ge(x_in[slot], use * 16)
                    after(pe, xT_done, g)
                    for k in range(ROWS):
                        mm = nc.tensor.transpose(ps_x[:, k * P:(k + 1) * P], x[slot][:, k * F:(k + 1) * F], const.ident[:, :])
                    mm.then_inc(x_turned, 1)
                    win.sum_windows(nc, pe, u, s, tiles(0), 0)
                    win.sum_windows(nc, pe, u, s, tiles(0), 1)
                if lag1:
                    pe.wait_ge(h1_done, g)
                    after(pe, h2_done, g - 1)
                    nc.tensor.matmul(ps_h2[:, :], const.w2[:, :], h1[:, :], start=True, stop=True).then_inc(mm2, 1)
                if lag2:
                    slot, _ = place(u, s - 2, 2)
                    pe.wait_ge(h2_done, g - 1)
                    after(pe, r_done, g - 2)
                    nc.tensor.matmul(ps_o[:, :], const.ones3[:, :], const.bias3[:, 0, :], start=True, stop=False)
                    for k in range(ROWS):
                        mm = nc.tensor.matmul(ps_o[:, k * F:(k + 1) * F], h2[slot][:, k * P:(k + 1) * P], const.w3[:, :],
                                              start=False, stop=k == ROWS - 1)
                    mm.then_inc(mm3, 1)
            quads(pe, step, 3)

        @block.scalar
        def _(act):
            def step(u, s, valid, tiles):
                g = UNROLL * u + s
                now, lag1, _, lag3 = valid
                if lag1:
                    act.wait_ge(mean_turned, g)
                    after(act, mm1, g - 1)
                    nc.scalar.activation(meanT[:, :].rearrange("f (k j q) -> f k j q", k=ROWS, j=NW), window_order(ps_mean[:, :]),
                                         ACT.Identity).then_inc(meanT_done, 1)
                    act.wait_ge(mm1, g)
                    after(act, mm2, g - 1)
                    nc.scalar.activation(h1[:, :], ps_h1[:, :], ACT.Relu, bias=const.b1[:, 0:1], scale=1.0).then_inc(h1_done, 1)
                if now:
                    slot, _ = place(u, s, 2)
                    act.wait_ge(x_turned, g + 1)
                    nc.scalar.activation(xT[slot][:, :], ps_x[:, :], ACT.Identity).then_inc(xT_done, 1)
                if lag3:
                    norm.deviations(nc, act, const, g - 3)
                    slot, use = place(u, s - 3, 2)
                    norm.normalise(nc, act, g - 3, out[slot], r[slot], stored[slot], use, out_done)
                    act.wait_ge(out_done, g - 2)
                    act.dma_start(rows_of(S["x1"], g - 3, F), out[slot][:, :]).then_inc(stored[slot], 16)
                if lag1:
                    slot, _ = place(u, s - 1, 2)
                    act.wait_ge(mm2, g)
                    after(act, mm3, g - 2)
                    nc.scalar.activation(h2[slot][:, :], ps_h2[:, :], ACT.Relu, bias=const.b2[:, 0:1], scale=1.0).then_inc(h2_done, 1)
            quads(act, step, 4, ahead=2)
            for s in range(2):
                act.wait_ge(stored[s], 16 * PAIRS)

        @block.vector
        def _(dve):
            win.hots(nc, dve, 0, 0, TPC)

            def step(u, s, valid, tiles):
                g = UNROLL * u + s
                early, now, _, _, lag3 = valid
                if lag3:
                    pair, _ = place(u, s - 3, 2)
                    slot, _ = place(u, s - 3, 4)
                    dve.wait_ge(mm3, g - 2)
                    after(dve, out_done, g - 4)
                    nc.vector.tensor_tensor(r[pair][:, :], ps_o[:, :], x[slot][:, :], ALU.add).then_inc(r_done, 1)
                    dve.wait_ge(r_done, g - 2)
                    norm.moments_of(nc, dve, r[pair], g - 3)
                if early:
                    win.hots(nc, dve, u, s + 1, tiles(-1))
                if lag3:
                    norm.scales(nc, dve, g - 3, out_done)
                if now:
                    win.hots_further(nc, dve, g)
                    win.means(nc, dve, g, mean_turned)
            quads(dve, step, 5, ahead=2, early=1)


def edges1(nc, ctx, A, S, const, tab):
    with ExitStack() as own:
        def sb(name, shape, dt=F32):
            return own.enter_context(nc.sbuf_tensor(f"e_{name}", shape, dt))

        def psum(name, parts=P):
            return own.enter_context(nc.psum_tensor(f"e_{name}", [parts, G], F32))

        def sem(name):
            return own.enter_context(nc.semaphore(f"e_{name}"))

        src = [sb(f"src{s}", [P, ROWS], I32) for s in range(2)]
        xs = [sb(f"xs{s}", [P, ROWS * F]) for s in range(2)]
        ea = [sb(f"ea{s}", [P, ROWS * FE]) for s in range(2)]
        xT = sb("xT", [P, G])
        eT = sb("eT", [FE, G])
        z = [sb(f"z{s}", [P, G]) for s in range(2)]
        stats = sb("stats", [P, NG, 6])
        ps_x = [psum(f"ps_x{s}") for s in range(2)]
        ps_e = [psum(f"ps_e{s}", FE) for s in range(2)]
        ps_z = [psum(f"ps_z{s}") for s in range(2)]

        src_in = [sem(f"src_in{s}") for s in range(2)]
        started = sem("started")
        xs_in = [sem(f"xs_in{s}") for s in range(2)]
        ea_in = [sem(f"ea_in{s}") for s in range(2)]
        x_turned, e_turned, xT_done, eT_done, mm, z_done, stats_done = (
            sem(k) for k in ("x_turned", "e_turned", "xT_done", "eT_done", "mm", "z_done", "stats_done"))
        stored = [sem(f"stored{s}") for s in range(2)]
        bn = BatchNormSems(sem)
        bn_bufs = batchnorm_buffers(sb, 1)
        block = own.enter_context(nc.Block())

        @block.sync
        def _(sp):
            def load(u, s, parts=P):
                g = 2 * u + s
                after(sp, x_turned, g - 1)
                rows = A["src"][g * G:g * G + parts * ROWS] if isinstance(g, int) else A["src"][bass.ds(g * G, parts * ROWS)]
                sp.dma_start(src[s][0:parts, :], rows.rearrange("(p k) -> p k", k=ROWS)).then_inc(src_in[s], 16)
                after(sp, e_turned, g - 1)
                sp.dma_start(ea[s][0:parts, :], rows_of(A["edge_attr_64"], g, FE, parts)).then_inc(ea_in[s], 16)
            for u in range(2):
                load(u, 0)
                load(u, 1)
            with sp.Fori(2, PAIRS - 1) as u:
                load(u, 0)
                load(u, 1)
            load(PAIRS - 1, 0)
            load(PAIRS - 1, 1, LAST)

        @block.gpsimd
        def _(pool):
            def step(u, s, valid):
                g = 2 * u + s
                pool.wait_ge(src_in[s], (u + 1) * 16)
                after(pool, x_turned, g - 1)
                pool.sem_inc(started, 1)
                for k in range(ROWS):
                    nc.gpsimd.indirect_dma_start(
                        out=xs[s][:, k * F:(k + 1) * F], out_offset=None, in_=S["x1"][:, :],
                        in_offset=bass.IndirectOffsetOnAxis(ap=src[s][:, k:k + 1], axis=0),
                        bounds_check=N - 1, oob_is_err=True).then_inc(xs_in[s], 16)
            steps(pool, step, 1)

        @block.tensor
        def _(pe):
            def step(u, s, valid):
                g = 2 * u + s
                now, lag1 = valid
                if now:
                    pe.wait_ge(ea_in[s], (u + 1) * 16)
                    after(pe, eT_done, g - 1)
                    pe.wait_ge(xs_in[s], (u + 1) * (16 * ROWS))
                    after(pe, xT_done, g - 1)
                    for k in range(ROWS):
                        op = nc.tensor.transpose(ps_x[s][:, k * P:(k + 1) * P], xs[s][:, k * F:(k + 1) * F], const.ident[:, :])
                    op.then_inc(x_turned, 1)
                    for k in range(ROWS):
                        op = nc.tensor.transpose(ps_e[s][:, k * P:(k + 1) * P], ea[s][:, k * FE:(k + 1) * FE], const.ident[:, :])
                    op.then_inc(e_turned, 1)
                if lag1:
                    pe.wait_ge(eT_done, g)
                    pe.wait_ge(xT_done, g)
                    after(pe, z_done, g - 2)
                    nc.tensor.matmul(ps_z[1 - s][:, :], const.v1x[:, :], xT[:, :], start=True, stop=False)
                    nc.tensor.matmul(ps_z[1 - s][:, :], const.v1e[:, :], eT[:, :], start=False, stop=True).then_inc(mm, 1)
            steps(pe, step, 2)

        @block.scalar
        def _(act):
            def step(u, s, valid):
                g = 2 * u + s
                now, lag1 = valid
                if now:
                    act.wait_ge(x_turned, g + 1)
                    after(act, mm, g)
                    nc.scalar.activation(xT[:, :], ps_x[s][:, :], ACT.Identity).then_inc(xT_done, 1)
                if lag1:
                    act.wait_ge(mm, g)
                    after(act, stats_done, g - 2)
                    if not isinstance(u, int) or g >= 3:
                        act.wait_ge(stored[1 - s], (u - 1 + s) * 16)
                    nc.scalar.activation(z[1 - s][:, :], ps_z[1 - s][:, :], ACT.Identity, bias=const.c1[:, 0:1], scale=1.0).then_inc(z_done, 1)
                    act.wait_ge(z_done, g)
                    act.dma_start(S["z"][bass.ds((g - 1) * P, P), :] if not isinstance(u, int) else S["z"][(g - 1) * P:g * P, :],
                                  z[1 - s][:, :]).then_inc(stored[1 - s], 16)
            steps(act, step, 2)
            for s in range(2):
                act.wait_ge(stored[s], 16 * PAIRS)
            batchnorm_act(nc, act, bn, bn_bufs, const)

        @block.vector
        def _(dve):
            def step(u, s, valid):
                g = 2 * u + s
                now, lag1 = valid
                if now:
                    dve.wait_ge(e_turned, g + 1)
                    after(dve, mm, g)
                    nc.vector.tensor_copy(eT[:, :], ps_e[s][:, :]).then_inc(eT_done, 1)
                if lag1:
                    dve.wait_ge(z_done, g)
                    whole = z[1 - s][:, :]
                    if isinstance(u, int) and g == NG:
                        whole = z[1 - s][:, :].rearrange("f (k p) -> f k p", k=ROWS)[:, :, 0:LAST]
                    to = stats[:, g - 1, :] if isinstance(u, int) else stats[:, bass.ds(g - 1, 1), :].rearrange("p a b -> p (a b)")
                    nc.vector.bn_stats(to, whole).then_inc(stats_done, 1)
            steps(dve, step, 2)
            dve.wait_ge(stats_done, NG)
            batchnorm_dve(nc, dve, bn, bn_bufs, [stats[:, :, :].rearrange("p g s -> p (g s)")],
                          [const.g1[:, 0:1]], [const.be1[:, 0:1]], const.s1, const.t1)


class BatchNormSems:
    def __init__(self, sem):
        self.aggr, self.std, self.scale, self.product, self.shift = (
            sem(k) for k in ("bn_aggr", "bn_std", "bn_scale", "bn_product", "bn_shift"))


def batchnorm_buffers(sb, n):
    return {"mv": sb("bn_mv", [P, n, 2]), "std": sb("bn_std", [P, n]), "inv": sb("bn_inv", [P, n]), "prod": sb("bn_prod", [P, n])}


def batchnorm_dve(nc, dve, bn, b, stats, gammas, betas, scale, shift):
    for m, st in enumerate(stats):
        op = nc.vector.bn_aggr(b["mv"][:, m, :], st)
    op.then_inc(bn.aggr, 1)
    dve.wait_ge(bn.std, 1)
    nc.vector.reciprocal(b["inv"][:, :], b["std"][:, :]).then_inc(bn.scale, 1)
    dve.wait_ge(bn.scale, 1)
    for m in range(len(stats)):
        op = nc.vector.tensor_tensor(scale[:, m:m + 1], b["inv"][:, m:m + 1], gammas[m], ALU.mult)
    op.then_inc(bn.scale, 1)
    dve.wait_ge(bn.scale, 2)
    for m in range(len(stats)):
        op = nc.vector.tensor_tensor(b["prod"][:, m:m + 1], b["mv"][:, m, 0:1], scale[:, m:m + 1], ALU.mult)
    op.then_inc(bn.product, 1)
    dve.wait_ge(bn.product, 1)
    for m in range(len(stats)):
        op = nc.vector.tensor_tensor(shift[:, m:m + 1], betas[m], b["prod"][:, m:m + 1], ALU.subtract)
    op.then_inc(bn.shift, 1)


def batchnorm_act(nc, act, bn, b, const):
    act.wait_ge(bn.aggr, 1)
    nc.scalar.activation(b["std"][:, :], b["mv"][:, :, 1], ACT.Sqrt, bias=const.eps[:, 0:1], scale=1.0).then_inc(bn.std, 1)


def messages1(nc, ctx, A, S, const, tab):
    with ExitStack() as own:
        def sb(name, shape, dt=F32):
            return own.enter_context(nc.sbuf_tensor(f"m_{name}", shape, dt))

        def sem(name):
            return own.enter_context(nc.semaphore(f"m_{name}"))

        z = [sb(f"z{s}", [P, G]) for s in range(2)]
        hT = [sb(f"hT{s}", [P, G]) for s in range(2)]
        h = [sb(f"h{s}", [P, ROWS * F]) for s in range(2)]
        ps = [own.enter_context(nc.psum_tensor(f"m_ps{s}", [P, G], F32)) for s in range(2)]
        z_in = [sem(f"z_in{s}") for s in range(2)]
        stored = [sem(f"stored{s}") for s in range(2)]
        hT_done, turned, h_done = (sem(k) for k in ("hT_done", "turned", "h_done"))
        block = own.enter_context(nc.Block())

        @block.sync
        def _(sp):
            def step(u, s, valid):
                g = 2 * u + s
                after(sp, hT_done, g - 1)
                sp.dma_start(z[s][:, :], S["z"][bass.ds(g * P, P), :] if not isinstance(u, int) else S["z"][g * P:(g + 1) * P, :]).then_inc(z_in[s], 16)
            steps(sp, step, 1)

        @block.scalar
        def _(act):
            def step(u, s, valid):
                g = 2 * u + s
                act.wait_ge(z_in[s], (u + 1) * 16)
                after(act, turned, g - 1)
                nc.scalar.activation(hT[s][:, :], z[s][:, :], ACT.Relu, bias=const.t1[:, 0:1], scale=const.s1[:, 0:1]).then_inc(hT_done, 1)
            steps(act, step, 1)

        @block.tensor
        def _(pe):
            def step(u, s, valid):
                g = 2 * u + s
                pe.wait_ge(hT_done, g + 1)
                after(pe, h_done, g - 1)
                for k in range(ROWS):
                    op = nc.tensor.transpose(ps[s][:, k * P:(k + 1) * P], hT[s][:, k * P:(k + 1) * P], const.ident[:, :])
                op.then_inc(turned, 1)
            steps(pe, step, 1)

        @block.vector
        def _(dve):
            def step(u, s, valid):
                g = 2 * u + s
                dve.wait_ge(turned, g + 1)
                after(dve, stored[s], u * 16)
                nc.vector.tensor_copy(h[s][:, :], ps[s][:, :]).then_inc(h_done, 1)
            steps(dve, step, 1)

        @block.gpsimd
        def _(pool):
            def step(u, s, valid):
                g = 2 * u + s
                pool.wait_ge(h_done, g + 1)
                pool.dma_start(rows_of(S["h"], g, F), h[s][:, :]).then_inc(stored[s], 16)
            steps(pool, step, 1)
            for s in range(2):
                pool.wait_ge(stored[s], 16 * PAIRS)


def nodes1(nc, ctx, A, S, const, tab):
    with ExitStack() as own:
        def sb(name, shape, dt=F32):
            return own.enter_context(nc.sbuf_tensor(f"n_{name}", shape, dt))

        def psum(name):
            return own.enter_context(nc.psum_tensor(f"n_{name}", [P, G], F32))

        def sem(name):
            return own.enter_context(nc.semaphore(f"n_{name}"))

        win = Windows(nc, own, "n", tab, const)
        x = [sb(f"x{s}", [P, ROWS * F]) for s in range(4)]
        xT = [sb(f"xT{s}", [P, G]) for s in range(2)]
        meanT = sb("meanT", [P, G])
        y = [sb(f"y{s}", [P, 2, G]) for s in range(2)]
        stats = sb("stats", [P, 2, NG, 6])
        ps_x, ps_mean, ps_y0, ps_y1 = (psum(k) for k in ("ps_x", "ps_mean", "ps_y0", "ps_y1"))
        ps_y = [ps_y0, ps_y1]
        x_in = [sem(f"x_in{s}") for s in range(4)]
        x_turned, mean_turned, xT_done, meanT_done, stats_done = (
            sem(k) for k in ("x_turned", "mean_turned", "xT_done", "meanT_done", "stats_done"))
        mm = [sem(f"mm{m}") for m in range(2)]
        y_done = [sem(f"y_done{m}") for m in range(2)]
        stored = [sem(f"stored{s}") for s in range(2)]
        bn = BatchNormSems(sem)
        bn_bufs = batchnorm_buffers(sb, 2)
        block = own.enter_context(nc.Block())

        @block.sync
        def _(sp):
            def step(u, s, valid, tiles):
                g = UNROLL * u + s
                now, _, lag2 = valid
                if now:
                    slot, _ = place(u, s, 4)
                    win.load(nc, sp, u, s, tiles(0), S["h"], S["dscr"])
                    after(sp, x_turned, g - 3)
                    sp.dma_start(x[slot][:, :], rows_of(S["x1"], g, F)).then_inc(x_in[slot], 16)
                if lag2:
                    win.load_further(nc, sp, g - 2, tiles(2), S["h"], S["dscr"])
            quads(sp, step, 3)

        @block.gpsimd
        def _(pool):
            win.ones(nc, pool)

            def step(u, s, valid, tiles):
                win.split(nc, pool, u, s, tiles(0))
                win.split_further(nc, pool, UNROLL * u + s)
            quads(pool, step, 1)

        @block.tensor
        def _(pe):
            pe.wait_ge(win.ones_done, 4)
            for s in range(2):
                pe.sem_inc(win.xsums_done[s], 1)

            def step(u, s, valid, tiles):
                g = UNROLL * u + s
                now, lag1 = valid
                if lag1:
                    slot, _ = place(u, s - 1, 2)
                    pe.wait_ge(win.mean_done, g)
                    after(pe, meanT_done, g - 1)
                    for j in range(NW):
                        op = nc.tensor.transpose(ps_mean[:, j * P:(j + 1) * P], win.mean[:, j, :], const.ident[:, :])
                    op.then_inc(mean_turned, 1)
                    pe.wait_ge(xT_done, g)
                    for m in range(2):
                        after(pe, y_done[m], g - 1)
                        nc.tensor.matmul(ps_y[m][:, :], const.v2[:, 0, m * P:(m + 1) * P], xT[slot][:, :], start=True, stop=False)
                    pe.wait_ge(meanT_done, g)
                    for m in range(2):
                        nc.tensor.matmul(ps_y[m][:, :], const.v2[:, 1, m * P:(m + 1) * P], meanT[:, :], start=False, stop=True).then_inc(mm[m], 1)
                if now:
                    slot, use = place(u, s, 4)
                    pe.wait_ge(x_in[slot], use * 16)
                    after(pe, xT_done, g)
                    for k in range(ROWS):
                        op = nc.tensor.transpose(ps_x[:, k * P:(k + 1) * P], x[slot][:, k * F:(k + 1) * F], const.ident[:, :])
                    op.then_inc(x_turned, 1)
                    win.sum_windows(nc, pe, u, s, tiles(0), 0)
                    win.sum_windows(nc, pe, u, s, tiles(0), 1)
            quads(pe, step, 2)

        @block.scalar
        def _(act):
            def step(u, s, valid, tiles):
                g = UNROLL * u + s
                now, lag1 = valid
                if lag1:
                    act.wait_ge(mean_turned, g)
                    after(act, mm[1], g - 1)
                    nc.scalar.activation(meanT[:, :].rearrange("f (k j q) -> f k j q", k=ROWS, j=NW), window_order(ps_mean[:, :]),
                                         ACT.Identity).then_inc(meanT_done, 1)
                    slot, use = place(u, s - 1, 2)
                    after(act, stats_done, g - 2)
                    after(act, stored[slot], (use - 1) * 16)
                    for m in range(2):
                        act.wait_ge(mm[m], g)
                        nc.scalar.activation(y[slot][:, m, :], ps_y[m][:, :], ACT.Identity, bias=const.c2[:, m:m + 1], scale=1.0).then_inc(y_done[m], 1)
                    for m in range(2):
                        act.wait_ge(y_done[m], g)
                    act.dma_start(panel(S["y"], g - 1), y[slot][:, :, :].rearrange("f m c -> f (m c)")).then_inc(stored[slot], 16)
                if now:
                    slot, _ = place(u, s, 2)
                    act.wait_ge(x_turned, g + 1)
                    nc.scalar.activation(xT[slot][:, :], ps_x[:, :], ACT.Identity).then_inc(xT_done, 1)
            quads(act, step, 2)
            for s in range(2):
                act.wait_ge(stored[s], 16 * PAIRS)
            batchnorm_act(nc, act, bn, bn_bufs, const)

        @block.vector
        def _(dve):
            win.hots(nc, dve, 0, 0, TPC)

            def step(u, s, valid, tiles):
                g = UNROLL * u + s
                early, now, lag1 = valid
                if early:
                    win.hots(nc, dve, u, s + 1, tiles(-1))
                if lag1:
                    slot, _ = place(u, s - 1, 2)
                    for m in range(2):
                        dve.wait_ge(y_done[m], g)
                        whole = y[slot][:, m, :]
                        if isinstance(u, int) and g == NG:
                            whole = whole.rearrange("f (k p) -> f k p", k=ROWS)[:, :, 0:LAST]
                        to = stats[:, m, g - 1, :] if isinstance(u, int) else stats[:, m, bass.ds(g - 1, 1), :].rearrange("p a b -> p (a b)")
                        op = nc.vector.bn_stats(to, whole)
                    op.then_inc(stats_done, 1)
                if now:
                    win.hots_further(nc, dve, g)
                    win.means(nc, dve, g, mean_turned)
            quads(dve, step, 3, early=1)
            dve.wait_ge(stats_done, NG)
            batchnorm_dve(nc, dve, bn, bn_bufs, [stats[:, m, :, :].rearrange("p g s -> p (g s)") for m in range(2)],
                          [const.g2[:, m:m + 1] for m in range(2)], [const.be2[:, m:m + 1] for m in range(2)], const.s2, const.t2)


def outputs1(nc, ctx, A, S, const, tab, result):
    with ExitStack() as own:
        def sb(name, shape, dt=F32):
            return own.enter_context(nc.sbuf_tensor(f"o_{name}", shape, dt))

        def sem(name):
            return own.enter_context(nc.semaphore(f"o_{name}"))

        y = [sb(f"y{s}", [P, 2 * G]) for s in range(4)]
        x = [sb(f"x{s}", [P, ROWS * F]) for s in range(4)]
        h = [sb(f"h{s}", [P, 2, G]) for s in range(2)]
        r = [sb(f"r{s}", [P, ROWS * F]) for s in range(2)]
        norm = Norm(sb, sem)
        out = [sb(f"out{s}", [P, ROWS * F]) for s in range(4)]
        ps_o = [own.enter_context(nc.psum_tensor(f"o_ps_o{s}", [P, G], F32)) for s in range(2)]
        y_in = [sem(f"y_in{s}") for s in range(4)]
        x_in = [sem(f"x_in{s}") for s in range(4)]
        stored = [sem(f"stored{s}") for s in range(4)]
        h_done, mm, r_done, out_done = (sem(k) for k in ("h_done", "mm", "r_done", "out_done"))
        block = own.enter_context(nc.Block())

        @block.sync
        def _(sp):
            def step(u, s, valid, tiles):
                g = UNROLL * u + s
                slot, _ = place(u, s, 4)
                after(sp, h_done, g - 3)
                sp.dma_start(y[slot][:, :], panel(S["y"], g)).then_inc(y_in[slot], 16)
                after(sp, r_done, g - 3)
                sp.dma_start(x[slot][:, :], rows_of(S["x1"], g, F)).then_inc(x_in[slot], 16)
            quads(sp, step, 1)

        @block.scalar
        def _(act):
            def step(u, s, valid, tiles):
                g = UNROLL * u + s
                now, _, lag2 = valid
                if lag2:
                    norm.deviations(nc, act, const, g - 2)
                if now:
                    slot, use = place(u, s, 4)
                    pair, _ = place(u, s, 2)
                    act.wait_ge(y_in[slot], use * 16)
                    after(act, mm, g - 1)
                    for m in range(2):
                        op = nc.scalar.activation(h[pair][:, m, :], y[slot][:, m * G:(m + 1) * G], ACT.Relu,
                                                  bias=const.t2[:, m:m + 1], scale=const.s2[:, m:m + 1])
                    op.then_inc(h_done, 1)
                if lag2:
                    pair, _ = place(u, s - 2, 2)
                    slot, use = place(u, s - 2, 4)
                    norm.normalise(nc, act, g - 2, out[slot], r[pair], stored[slot], use, out_done)
            quads(act, step, 3, ahead=2)

        @block.tensor
        def _(pe):
            def step(u, s, valid, tiles):
                g = UNROLL * u + s
                pair, _ = place(u, s, 2)
                pe.wait_ge(h_done, g + 1)
                after(pe, r_done, g - 1)
                nc.tensor.matmul(ps_o[pair][:, :], const.ones3[:, :], const.bias3[:, 1, :], start=True, stop=False)
                for k in range(ROWS):
                    for m in range(2):
                        op = nc.tensor.matmul(ps_o[pair][:, k * F:(k + 1) * F], h[pair][:, m, k * P:(k + 1) * P], const.vl[:, m, :],
                                              start=False, stop=k == ROWS - 1 and m == 1)
                op.then_inc(mm, 1)
            quads(pe, step, 1)

        @block.vector
        def _(dve):
            def step(u, s, valid, tiles):
                g = UNROLL * u + s
                _, lag1, lag2 = valid
                if lag2:
                    norm.scales(nc, dve, g - 2, out_done)
                if lag1:
                    slot, use = place(u, s - 1, 4)
                    pair, _ = place(u, s - 1, 2)
                    dve.wait_ge(mm, g)
                    dve.wait_ge(x_in[slot], use * 16)
                    after(dve, out_done, g - 2)
                    nc.vector.scalar_tensor_tensor(out=r[pair][:, :], in0=ps_o[pair][:, :], scalar=0.0, in1=x[slot][:, :],
                                                   op0=ALU.max, op1=ALU.add).then_inc(r_done, 1)
                    dve.wait_ge(r_done, g)
                    norm.moments_of(nc, dve, r[pair], g - 1)
            quads(dve, step, 3, ahead=2)

        @block.gpsimd
        def _(pool):
            def step(u, s, valid, tiles):
                g = UNROLL * u + s
                slot, _ = place(u, s, 4)
                parts = LAST if isinstance(g, int) and g == NG - 1 else P
                pool.wait_ge(out_done, g + 1)
                pool.dma_start(rows_of(result, g, F, parts), out[slot][0:parts, :]).then_inc(stored[slot], 16)
            quads(pool, step, 1)
            for s in range(4):
                pool.wait_ge(stored[s], 16 * len(range(s, NG, 4)))


def build(nc, A, result):
    with ExitStack() as ctx:
        ctx.enter_context(nc.allow_non_contiguous_dma(reason="single columns of weights and tables"))

        def sb(name, shape, dt=F32):
            return ctx.enter_context(nc.sbuf_tensor(name, shape, dt))

        S = {
            "x1": nc.dram_tensor("s_x1", (NPAD, F), F32).ap(),
            "h": nc.dram_tensor("s_h", (NPAD, F), F32).ap(),
            "z": nc.dram_tensor("s_z", (NG * P, G), F32).ap(),
            "y": nc.dram_tensor("s_y", (NG * P, 2 * G), F32).ap(),
            "dscr": nc.dram_tensor("s_dst", (DSCR, 1), F32).ap(),
            "tabs": nc.dram_tensor("s_tabs", (2, TABW), I32).ap(),
        }
        c = Constants()
        c.ident = sb("ident", [P, P])
        c.node = sb("node", [P, NW, WIN], F16)
        c.minus_first = sb("minus_first", [P, NG])
        c.node_w = sb("node_w", [P, WIN], BF16)
        c.window_first = sb("window_first", [P, NG * NW])
        c.near = sb("near", [P, NG * NW, TPC])
        c.brow = sb("brow", [3, 2, F])
        c.bias3 = sb("bias3", [3, 2, ROWS * F], BF16)
        c.ones3 = sb("ones3", [3, P], BF16)
        c.eps = sb("eps", [P, 1])
        c.w1, c.w2, c.w3 = sb("w1", [P, 2, F]), sb("w2", [P, F]), sb("w3", [P, F])
        c.b1, c.b2 = sb("b1", [P, 1]), sb("b2", [P, 1])
        c.v1x, c.v1e = sb("v1x", [P, F]), sb("v1e", [FE, F])
        c.c1, c.g1, c.be1 = sb("c1", [P, 1]), sb("g1", [P, 1]), sb("be1", [P, 1])
        c.s1, c.t1 = sb("s1", [P, 1]), sb("t1", [P, 1])
        c.v2, c.vl = sb("v2", [P, 2, 2 * F]), sb("vl", [P, 2, F])
        c.c2, c.g2, c.be2 = sb("c2", [P, 2]), sb("g2", [P, 2]), sb("be2", [P, 2])
        c.s2, c.t2 = sb("s2", [P, 2]), sb("t2", [P, 2])
        tab = sb("tab", [1, TAB], I32)

        def column(a):
            return a.rearrange("(m p) -> p m", p=P)

        def blocks(a):
            return a.rearrange("(b p) f -> p b f", p=P)

        c.loads = [
            (c.w1[:, :, :], blocks(A["L0_gnn_W1"])), (c.w2[:, :], A["L0_gnn_W2"]), (c.w3[:, :], A["L0_gnn_W3"]),
            (c.b1[:, :], column(A["L0_gnn_b1"])), (c.b2[:, :], column(A["L0_gnn_b2"])),
            (c.v1x[:, :], A["L1_gnn_W1"][0:F, :]), (c.v1e[:, :], A["L1_gnn_W1"][F:F + FE, :]),
            (c.c1[:, :], column(A["L1_gnn_b1"])), (c.g1[:, :], column(A["L1_gnn_g1"])), (c.be1[:, :], column(A["L1_gnn_be1"])),
            (c.v2[:, :, :], blocks(A["L1_gnn_W2"])), (c.vl[:, :, :], blocks(A["L1_gnn_Wl"])),
            (c.c2[:, :], column(A["L1_gnn_b2"])), (c.g2[:, :], column(A["L1_gnn_g2"])), (c.be2[:, :], column(A["L1_gnn_be2"])),
        ]
        for p in range(3):
            for m, name in enumerate(("L0_gnn_b3", "L1_gnn_bl")):
                c.loads.append((c.brow[p:p + 1, m, :], A[name].rearrange("(o f) -> o f", o=1)))
        with nc.Block() as block:
            @block.vector
            def _(dve):
                nc.vector.memset(c.eps[:, :], EPS)
        prepare(nc, ctx, A, S, c, tab)
        layer0(nc, ctx, A, S, c, tab)
        edges1(nc, ctx, A, S, c, tab)
        messages1(nc, ctx, A, S, c, tab)
        nodes1(nc, ctx, A, S, c, tab)
        outputs1(nc, ctx, A, S, c, tab, result)


_INS = ["x", "src", "dst", "edge_attr_128", "edge_attr_64", "L0_gnn_W1", "L0_gnn_b1", "L0_gnn_W2", "L0_gnn_b2",
        "L0_gnn_W3", "L0_gnn_b3", "L1_gnn_W1", "L1_gnn_b1", "L1_gnn_g1", "L1_gnn_be1", "L1_gnn_W2", "L1_gnn_b2",
        "L1_gnn_g2", "L1_gnn_be2", "L1_gnn_Wl", "L1_gnn_bl"]


def kernel(**inputs):
    import numpy as np
    import concourse.bacc as bacc
    from concourse.bass_utils import run_bass_kernel_spmd

    nc = bacc.Bacc("TRN2", target_bir_lowering=False, num_devices=1)
    arrays, args = {}, {}
    for name in _INS:
        a = np.ascontiguousarray(inputs[name])
        arrays[f"in_{name}"] = a
        args[name] = nc.dram_tensor(f"in_{name}", a.shape, mybir.dt.from_np(a.dtype), kind="ExternalInput").ap()
    result = nc.dram_tensor("out", (N, F), F32, kind="ExternalOutput").ap()
    build(nc, args, result)
    r = run_bass_kernel_spmd(nc, [arrays], core_ids=[0])
    return r.results[0]["out"]
```
